# Optimizing a Trainium2 kernel written in Bass

```python
import numpy as np
import jax
import jax.numpy as jnp

def _softmax(x, axis=-1):
    return jax.nn.softmax(x, axis=axis)

def _gelu(x):
    return jax.nn.gelu(x, approximate=True)

def _silu(x):
    return jax.nn.silu(x)

def _sigmoid(x):
    return jax.nn.sigmoid(x)

def _layernorm(x, axis=-1, eps=1e-05):
    m = jnp.mean(x, axis=axis, keepdims=True)
    v = jnp.var(x, axis=axis, keepdims=True)
    return (x - m) / jnp.sqrt(v + eps)

def _scatter_add(tgt, idx, src, axis=0):
    return tgt.at[idx].add(src)

def _segment_sum(src, seg, n):
    return jax.ops.segment_sum(src, seg, n)
kernel_name = 'mk_xattn_seq_d2_seqx_r4_7daf2f'

def setup_inputs(seed: int=0):
    np.random.seed(seed)
    _w = jnp.asarray

    def _rec_inputs():
        import jax
        import jax.numpy as jnp
        _rk = jax.random.key(seed)
        x = -0.0002928 + 1 * jax.random.normal(jax.random.fold_in(_rk, 1), (8, 256, 512), jnp.float32)
        _lenS = 256 - jax.random.randint(jax.random.fold_in(_rk, 7), (8,), 0, max(1, 256 // 4) + 1, jnp.int32)
        _lenS2 = 256 - jax.random.randint(jax.random.fold_in(_rk, 8), (8,), 0, max(1, 256 // 4) + 1, jnp.int32)
        _ctx_2048P = jax.random.normal(jax.random.fold_in(_rk, 11), (8, 16, 512), jnp.float32)
        _ctx_2048c = jax.random.dirichlet(jax.random.fold_in(_rk, 511), 0.3 * jnp.ones((16,), jnp.float32), (8, 256))
        _ctx_2048t = jnp.einsum('bsk,bkd->bsd', _ctx_2048c, _ctx_2048P)
        _ctx_2048t = _ctx_2048t * jax.lax.rsqrt(jnp.mean(jnp.square(_ctx_2048t)) + 1e-12) * 0.953939
        ctx_2048 = -1.39393e-06 + 0.999914 * (_ctx_2048t + 0.3 * jax.random.normal(jax.random.fold_in(_rk, 611), (8, 256, 512), jnp.float32))
        _validS = jnp.arange(256)[None, :] < _lenS[:, None]
        _validS2 = jnp.arange(256)[None, :] < _lenS2[:, None]
        _causal = jnp.tril(jnp.ones((256, 256), dtype=bool))
        mask_1x1xSxS2_fc1 = jnp.where(jnp.broadcast_to(_validS2[0:1, None, None, :], (1, 1, 256, 256)), 1.0, 0.0).astype(jnp.float32)
        mask_Bx1xSxS2_ff1 = jnp.where(jnp.ones((8, 1, 256, 256), dtype=bool), 1.0, 0.0).astype(jnp.float32)
        mask_Bx1x2048_bf1 = jnp.ones((8, 1, 512), dtype=bool)
        return (x, ctx_2048, mask_1x1xSxS2_fc1, mask_Bx1xSxS2_ff1, mask_Bx1x2048_bf1)
    x, ctx_2048, mask_1x1xSxS2_fc1, mask_Bx1xSxS2_ff1, mask_Bx1x2048_bf1 = _rec_inputs()

    def _L0_xattn_setup():
        import jax, jax.numpy as jnp
        import numpy as np
        H = 512
        NH = 16
        HD = H // NH
        EPS = 1e-05

        def gelu(x):
            return 0.5 * x * (1.0 + jnp.tanh(0.7978845608028654 * x * (1.0 + 0.044715 * x * x)))

        def layernorm(x, scale, bias):
            m = jnp.mean(x, axis=-1, keepdims=True)
            v = jnp.mean(jnp.square(x - m), axis=-1, keepdims=True)
            return (x - m) * jax.lax.rsqrt(v + EPS) * scale + bias

        def split_heads(x):
            b, s, _ = x.shape
            return x.reshape(b, s, NH, HD).transpose(0, 2, 1, 3)

        def merge_heads(x):
            b, nh, s, hd = x.shape
            return x.transpose(0, 2, 1, 3).reshape(b, s, nh * hd)

        def attention(q, k, v, mask):
            scores = jnp.einsum('bhqd,bhkd->bhqk', q, k) / jnp.sqrt(jnp.float32(HD))
            scores = scores * mask - 10000.0 * (1.0 - mask)
            probs = jax.nn.softmax(scores, axis=-1)
            return jnp.einsum('bhqk,bhkd->bhqd', probs, v)
        key = jax.random.key(seed)
        ks = jax.random.split(key, 16)
        b, s, t = (2, 256, 256)
        w = lambda k, i, o: jax.random.normal(k, (i, o), jnp.float32) * 0.02
        inp = {'hidden_states': jax.random.normal(ks[0], (b, s, H), jnp.float32), 'encoder_states': jax.random.normal(ks[1], (b, t, H), jnp.float32), 'ltor_mask': jnp.tril(jnp.ones((1, 1, s, s), jnp.float32)), 'cross_mask': jnp.ones((b, 1, s, t), jnp.float32), 'ln1_s': jnp.ones((H,), jnp.float32), 'ln1_b': jnp.zeros((H,), jnp.float32), 'w_qkv': w(ks[2], H, 3 * H), 'b_qkv': jnp.zeros((3 * H,), jnp.float32), 'w_ao': w(ks[3], H, H), 'b_ao': jnp.zeros((H,), jnp.float32), 'ln2_s': jnp.ones((H,), jnp.float32), 'ln2_b': jnp.zeros((H,), jnp.float32), 'w_q': w(ks[4], H, H), 'b_q': jnp.zeros((H,), jnp.float32), 'w_kv': w(ks[5], H, 2 * H), 'b_kv': jnp.zeros((2 * H,), jnp.float32), 'w_co': w(ks[6], H, H), 'b_co': jnp.zeros((H,), jnp.float32), 'ln3_s': jnp.ones((H,), jnp.float32), 'ln3_b': jnp.zeros((H,), jnp.float32), 'w1': w(ks[7], H, 4 * H), 'b1': jnp.zeros((4 * H,), jnp.float32), 'w2': w(ks[8], 4 * H, H), 'b2': jnp.zeros((H,), jnp.float32)}
        return inp
    _L0_xattn_all = _L0_xattn_setup()
    _L0_xattn_in = {k: v for k, v in _L0_xattn_all.items() if k in ('ln1_s', 'ln1_b', 'w_qkv', 'b_qkv', 'w_ao', 'b_ao', 'ln2_s', 'ln2_b', 'w_q', 'b_q', 'w_kv', 'b_kv', 'w_co', 'b_co', 'ln3_s', 'ln3_b', 'w1', 'b1', 'w2', 'b2')}
    del _L0_xattn_all

    def _L1_xattn_setup():
        import jax, jax.numpy as jnp
        import numpy as np
        import math
        N_HEADS = 16
        EPS = 1e-05

        def _masked_instance_norm(x, mask):
            m = mask.astype(x.dtype)
            x = x * m
            n_valid = jnp.sum(m, axis=-1, keepdims=True)
            mean = jnp.sum(x, axis=-1, keepdims=True) / n_valid
            var = jnp.sum(x * x, axis=-1, keepdims=True) / n_valid - mean * mean
            x = (x - mean) / jnp.sqrt(jax.nn.relu(var) + EPS)
            return x * m
        key = jax.random.key(seed)
        ks = jax.random.split(key, 8)
        bs, c, t1, t2 = (2, 256, 512, 512)
        s = 1.0 / math.sqrt(c)
        return {'x': jax.random.normal(ks[0], (bs, c, t1), jnp.float32), 'mask': jnp.ones((bs, 1, t1), jnp.bool_), 'kv': jax.random.normal(ks[1], (bs, c, t2), jnp.float32), 'kv_mask': jnp.ones((bs, 1, t2), jnp.bool_), 'Wq': jax.random.normal(ks[2], (c, c), jnp.float32) * s, 'bq': jnp.zeros((c,), jnp.float32), 'Wk': jax.random.normal(ks[3], (c, c), jnp.float32) * s, 'bk': jnp.zeros((c,), jnp.float32), 'Wv': jax.random.normal(ks[4], (c, c), jnp.float32) * s, 'bv': jnp.zeros((c,), jnp.float32)}
    _L1_xattn_all = _L1_xattn_setup()
    _L1_xattn_in = {k: v for k, v in _L1_xattn_all.items() if k in ('Wq', 'bq', 'Wk', 'bk', 'Wv', 'bv')}
    del _L1_xattn_all
    return {'x': x, 'ctx_2048': ctx_2048, 'mask_1x1xSxS2_fc1': mask_1x1xSxS2_fc1, 'mask_Bx1xSxS2_ff1': mask_Bx1xSxS2_ff1, 'mask_Bx1x2048_bf1': mask_Bx1x2048_bf1, 'L0_xattn_ln1_s': _L0_xattn_in['ln1_s'], 'L0_xattn_ln1_b': _L0_xattn_in['ln1_b'], 'L0_xattn_w_qkv': _L0_xattn_in['w_qkv'], 'L0_xattn_b_qkv': _L0_xattn_in['b_qkv'], 'L0_xattn_w_ao': _L0_xattn_in['w_ao'], 'L0_xattn_b_ao': _L0_xattn_in['b_ao'], 'L0_xattn_ln2_s': _L0_xattn_in['ln2_s'], 'L0_xattn_ln2_b': _L0_xattn_in['ln2_b'], 'L0_xattn_w_q': _L0_xattn_in['w_q'], 'L0_xattn_b_q': _L0_xattn_in['b_q'], 'L0_xattn_w_kv': _L0_xattn_in['w_kv'], 'L0_xattn_b_kv': _L0_xattn_in['b_kv'], 'L0_xattn_w_co': _L0_xattn_in['w_co'], 'L0_xattn_b_co': _L0_xattn_in['b_co'], 'L0_xattn_ln3_s': _L0_xattn_in['ln3_s'], 'L0_xattn_ln3_b': _L0_xattn_in['ln3_b'], 'L0_xattn_w1': _L0_xattn_in['w1'], 'L0_xattn_b1': _L0_xattn_in['b1'], 'L0_xattn_w2': _L0_xattn_in['w2'], 'L0_xattn_b2': _L0_xattn_in['b2'], 'L1_xattn_Wq': _L1_xattn_in['Wq'], 'L1_xattn_bq': _L1_xattn_in['bq'], 'L1_xattn_Wk': _L1_xattn_in['Wk'], 'L1_xattn_bk': _L1_xattn_in['bk'], 'L1_xattn_Wv': _L1_xattn_in['Wv'], 'L1_xattn_bv': _L1_xattn_in['bv']}

def reference(x, ctx_2048, mask_1x1xSxS2_fc1, mask_Bx1xSxS2_ff1, mask_Bx1x2048_bf1, L0_xattn_ln1_s, L0_xattn_ln1_b, L0_xattn_w_qkv, L0_xattn_b_qkv, L0_xattn_w_ao, L0_xattn_b_ao, L0_xattn_ln2_s, L0_xattn_ln2_b, L0_xattn_w_q, L0_xattn_b_q, L0_xattn_w_kv, L0_xattn_b_kv, L0_xattn_w_co, L0_xattn_b_co, L0_xattn_ln3_s, L0_xattn_ln3_b, L0_xattn_w1, L0_xattn_b1, L0_xattn_w2, L0_xattn_b2, L1_xattn_Wq, L1_xattn_bq, L1_xattn_Wk, L1_xattn_bk, L1_xattn_Wv, L1_xattn_bv):
    import jax
    import jax.numpy as jnp

    def _L0_xattn_ref(hidden_states, encoder_states, ltor_mask, cross_mask, ln1_s, ln1_b, w_qkv, b_qkv, w_ao, b_ao, ln2_s, ln2_b, w_q, b_q, w_kv, b_kv, w_co, b_co, ln3_s, ln3_b, w1, b1, w2, b2):
        import jax, jax.numpy as jnp
        import numpy as np
        H = 512
        NH = 16
        HD = H // NH
        EPS = 1e-05

        def gelu(x):
            return 0.5 * x * (1.0 + jnp.tanh(0.7978845608028654 * x * (1.0 + 0.044715 * x * x)))

        def layernorm(x, scale, bias):
            m = jnp.mean(x, axis=-1, keepdims=True)
            v = jnp.mean(jnp.square(x - m), axis=-1, keepdims=True)
            return (x - m) * jax.lax.rsqrt(v + EPS) * scale + bias

        def split_heads(x):
            b, s, _ = x.shape
            return x.reshape(b, s, NH, HD).transpose(0, 2, 1, 3)

        def merge_heads(x):
            b, nh, s, hd = x.shape
            return x.transpose(0, 2, 1, 3).reshape(b, s, nh * hd)

        def attention(q, k, v, mask):
            scores = jnp.einsum('bhqd,bhkd->bhqk', q, k) / jnp.sqrt(jnp.float32(HD))
            scores = scores * mask - 10000.0 * (1.0 - mask)
            probs = jax.nn.softmax(scores, axis=-1)
            return jnp.einsum('bhqk,bhkd->bhqd', probs, v)
        ln_out = layernorm(hidden_states, ln1_s, ln1_b)
        qkv = ln_out @ w_qkv + b_qkv
        q, k, v = jnp.split(qkv, 3, axis=-1)
        ctx = merge_heads(attention(split_heads(q), split_heads(k), split_heads(v), ltor_mask))
        attn_out = ctx @ w_ao + b_ao
        x = hidden_states + attn_out
        ln_out = layernorm(x, ln2_s, ln2_b)
        q = ln_out @ w_q + b_q
        kv = encoder_states @ w_kv + b_kv
        k, v = jnp.split(kv, 2, axis=-1)
        ctx = merge_heads(attention(split_heads(q), split_heads(k), split_heads(v), cross_mask))
        cross_out = ctx @ w_co + b_co
        x = x + cross_out
        ln_out = layernorm(x, ln3_s, ln3_b)
        mlp_out = gelu(ln_out @ w1 + b1) @ w2 + b2
        return x + mlp_out

    def _L1_xattn_ref(x, mask, kv, kv_mask, Wq, bq, Wk, bk, Wv, bv):
        import jax, jax.numpy as jnp
        import numpy as np
        import math
        N_HEADS = 16
        EPS = 1e-05

        def _masked_instance_norm(x, mask):
            m = mask.astype(x.dtype)
            x = x * m
            n_valid = jnp.sum(m, axis=-1, keepdims=True)
            mean = jnp.sum(x, axis=-1, keepdims=True) / n_valid
            var = jnp.sum(x * x, axis=-1, keepdims=True) / n_valid - mean * mean
            x = (x - mean) / jnp.sqrt(jax.nn.relu(var) + EPS)
            return x * m
        bs, c, t1 = x.shape
        h = N_HEADS
        d = c // h
        scale = 1.0 / math.sqrt(d)
        q = jnp.einsum('oc,bct->bot', Wq, x) + bq[None, :, None]
        k = jnp.einsum('oc,bct->bot', Wk, kv) + bk[None, :, None]
        v = jnp.einsum('oc,bct->bot', Wv, kv) + bv[None, :, None]
        q = q.reshape(bs, h, d, t1).transpose(0, 1, 3, 2)
        k = k.reshape(bs, h, d, -1)
        v = v.reshape(bs, h, d, -1).transpose(0, 1, 3, 2)
        attn = jnp.einsum('bhqd,bhdk->bhqk', q * scale, k)
        attn = jnp.where(kv_mask[:, :, None, :], attn, -jnp.inf)
        attn = jax.nn.softmax(attn, axis=-1)
        mean = jnp.einsum('bhqk,bhkd->bhqd', attn, v)
        ex2 = jnp.einsum('bhqk,bhkd->bhqd', attn, v * v)
        std = jnp.sqrt(jax.nn.relu(ex2 - mean * mean))
        mean = mean.transpose(0, 1, 3, 2).reshape(bs, c, t1)
        std = std.transpose(0, 1, 3, 2).reshape(bs, c, t1)
        xn = _masked_instance_norm(x, mask)
        out = (xn * std + mean) * mask.astype(x.dtype)
        return out
    x = _L0_xattn_ref(x, ctx_2048, mask_1x1xSxS2_fc1, mask_Bx1xSxS2_ff1, L0_xattn_ln1_s, L0_xattn_ln1_b, L0_xattn_w_qkv, L0_xattn_b_qkv, L0_xattn_w_ao, L0_xattn_b_ao, L0_xattn_ln2_s, L0_xattn_ln2_b, L0_xattn_w_q, L0_xattn_b_q, L0_xattn_w_kv, L0_xattn_b_kv, L0_xattn_w_co, L0_xattn_b_co, L0_xattn_ln3_s, L0_xattn_ln3_b, L0_xattn_w1, L0_xattn_b1, L0_xattn_w2, L0_xattn_b2)
    x = _L1_xattn_ref(x, mask_Bx1x2048_bf1, ctx_2048, mask_Bx1x2048_bf1, L1_xattn_Wq, L1_xattn_bq, L1_xattn_Wk, L1_xattn_bk, L1_xattn_Wv, L1_xattn_bv)
    return x

_drawn_inputs = setup_inputs


def setup_inputs(seed=0):
    import zlib

    import numpy as np

    out = dict(_drawn_inputs(seed))
    spreads = {'L0_xattn_ln1_s': (1.0, 0.6),
     'L0_xattn_ln1_b': (0.0, 0.397),
     'L0_xattn_b_qkv': (0.0, 0.1),
     'L0_xattn_b_ao': (0.0, 0.1),
     'L0_xattn_ln2_s': (1.0, 0.6),
     'L0_xattn_ln2_b': (0.0, 0.8),
     'L0_xattn_b_q': (0.0, 2.0),
     'L0_xattn_b_kv': (0.0, 0.1),
     'L0_xattn_b_co': (0.0, 0.1),
     'L0_xattn_ln3_s': (1.0, 0.2),
     'L0_xattn_ln3_b': (0.0, 0.322),
     'L0_xattn_b1': (0.0, 0.1),
     'L0_xattn_b2': (0.0, 0.1),
     'L1_xattn_bq': (0.0, 0.1),
     'L1_xattn_bk': (0.0, 2.0),
     'L1_xattn_bv': (0.0, 0.1)}
    factors = {'L0_xattn_w_q': 7.345}
    for name, (base, spread) in spreads.items():
        noise = np.random.default_rng([zlib.crc32(name.encode()), seed]).standard_normal(out[name].shape)
        drawn = base * np.exp(spread * noise) if base else spread * noise
        out[name] = jnp.asarray(drawn.astype(out[name].dtype))
    for name, factor in factors.items():
        out[name] = (out[name] * factor).astype(out[name].dtype)
    return out
```

```python
import concourse.bass as bass
from concourse import mybir
from contextlib import ExitStack

F32 = mybir.dt.float32
F32R = mybir.dt.float32r
U8 = mybir.dt.uint8
ALU = mybir.AluOpType
ACT = mybir.ActivationFunctionType
AX = mybir.AxisListType

P = 128
B, S, H = 8, 256, 512
NT = S // P
KT = H // P
NH, HD = 16, 32
HPG = P // HD
F = 4 * H
EPS = 1e-5
DMA = 16


def counted_to(engine, value):
    return value if isinstance(value, int) else engine.to_reg(value)


def attention_phase(nc, name, cross, x_in, x_out, context, mask, w_qkv, w_out, bias_qk, bias_v,
                    bias_o, ln_s, ln_b):
    NQK = 8
    PAIRS = NH // 2
    GROUPS = NH // HPG
    STACK_DMAS = 2 * 3 * HPG
    QK_SLOTS = (3, 4, 5, 6) if cross else (2, 3, 5, 6)
    CHUNKS = [(0, (0, 1)), (1, (0, 1)), (0, (2, 3)), (1, (2, 3))]
    with ExitStack() as ctx:
        sems = []

        def sb(n, shape, dtype=F32):
            return ctx.enter_context(nc.sbuf_tensor(f"{name}_{n}", shape, dtype))

        def pb(n, shape):
            return ctx.enter_context(nc.psum_tensor(f"{name}_{n}", shape, F32))

        def sem(n):
            sems.append(nc.alloc_semaphore(f"{name}_{n}"))
            return sems[-1]

        w_hi = sb("w_hi", [P, KT, 3 * H], F32R)
        w_lo = sb("w_lo", [P, KT, 3 * H], F32R)
        wo_hi = sb("wo_hi", [P, KT, H], F32R)
        wo_lo = sb("wo_lo", [P, KT, H], F32R)
        bqk = sb("bqk", [P, NQK])
        bv_row = sb("bv_row", [P, H])
        bo_row = sb("bo_row", [P, H])
        lns = sb("lns", [P, KT])
        lnb = sb("lnb", [P, KT])
        ident = sb("ident", [P, P])
        neg_half = sb("neg_half", [P, NT])
        x_ln = sb("x_ln", [P, NT, H])
        x_res = sb("x_res", [P, NT, H])
        stats = sb("stats", [P, NT, 6])
        mean_var = sb("mean_var", [P, NT, 2])
        rstd = sb("rstd", [P, NT])
        y = sb("y", [P, KT, S])
        y_hi = sb("y_hi", [P, KT, S], F32R)
        y_lo = sb("y_lo", [P, KT, S], F32R)
        if cross:
            c_nat = sb("c_nat", [P, NT, H])
            c_hi = sb("c_hi", [P, KT, S], F32R)
            c_lo = sb("c_lo", [P, KT, S], F32R)
        qk_hi = sb("qk_hi", [P, NQK, S], F32R)
        qk_lo = sb("qk_lo", [P, NQK, S], F32R)
        q_stack = sb("q_stack", [P, NH, S], F32R)
        k_stack = sb("k_stack", [P, NH, S], F32R)
        v = sb("v", [P, NT, H])
        mask_raw = sb("mask_raw", [P, NT, S])
        mask_mul = sb("mask_mul", [P, NT, S])
        mask_add = sb("mask_add", [P, NT, S])
        NS = 4
        sc = sb("sc", [P, NS, 2, NT, S])
        neg_max = sb("neg_max", [P, NS, 2, NT])
        sums = sb("sums", [P, 2, NT, HPG])
        recip = sb("recip", [P, 2, NT, HPG])
        recip_b = sb("recip_b", [P, NT, HPG, HD])
        probs_t = sb("probs_t", [P, 2, HPG, NT, S])
        recip_t = sb("recip_t", [P, S])
        cx = sb("cx", [P, GROUPS, S])
        cx_hi = sb("cx_hi", [P, GROUPS, S], F32R)
        cx_lo = sb("cx_lo", [P, GROUPS, S], F32R)
        stage = [probs_t[:, i, :, :, :].rearrange("p h t s -> p (h t s)")
                 .rearrange("p (k n) -> p k n", k=KT) for i in range(2)]

        ps_s = pb("ps_s", [P, 2, NT, S])
        ps_t = pb("ps_t", [P, 2, NT, S])
        ps_r = pb("ps_r", [P, 2 * S])
        ps_c = pb("ps_c", [P, 2 * S])
        ps_p = pb("ps_p", [P, 2, H])
        ps_p4 = ps_p[:, :, :].rearrange("p b (k s) -> p (b k) s", k=2)

        consts_loaded = sem("consts_loaded")
        w_loaded = [sem(f"w_loaded{i}") for i in range(2)]
        w_hi_made, w_lo_made = sem("w_hi_made"), sem("w_lo_made")
        ident_made = sem("ident_made")
        x_loaded, res_loaded, stored = sem("x_loaded"), sem("res_loaded"), sem("stored")
        c_loaded, c_turned = sem("c_loaded"), sem("c_turned")
        c_copied, c_hi_made, c_lo_made = sem("c_copied"), sem("c_hi_made"), sem("c_lo_made")
        mask_loaded, mask_made, mask_mul_made = sem("mask_loaded"), sem("mask_made"), sem("mask_mul_made")
        stats_made, mv_made = sem("stats_made"), sem("mv_made")
        var_made, rstd_made = sem("var_made"), sem("rstd_made")
        z_made, turned, y_made = sem("z_made"), sem("turned"), sem("y_made")
        y_hi_made, y_lo_made = sem("y_hi_made"), sem("y_lo_made")
        qk_summed, qk_hi_made, qk_lo_made = sem("qk_summed"), sem("qk_hi_made"), sem("qk_lo_made")
        stacked = [sem(f"stacked{i}") for i in range(2)]
        v_summed, v_made = sem("v_summed"), sem("v_made")
        scored, multiplied, masked = sem("scored"), sem("multiplied"), sem("masked")
        exped, probs_turned, probs_made = sem("exped"), sem("probs_turned"), sem("probs_made")
        recip_made, recip_spread = sem("recip_made"), sem("recip_spread")
        recip_turned, recip_copied = sem("recip_turned"), sem("recip_copied")
        pv_summed, cx_made = sem("pv_summed"), sem("cx_made")
        cx_hi_made, cx_lo_made = sem("cx_hi_made"), sem("cx_lo_made")
        o_summed, res_biased, x_made = sem("o_summed"), sem("res_biased"), sem("x_made")

        WCHUNKS = 4
        NCONST = 5

        with nc.Block() as block:

            @block.sync
            def _(sp):
                def load_x(b):
                    sp.dma_start(x_ln[:, :, :], x_in[b].rearrange("(j p) d -> p j d", p=P)
                                 ).then_inc(x_loaded, DMA)

                def load_c(b):
                    sp.dma_start(c_nat[:, :, :], context[b].rearrange("(j p) d -> p j d", p=P)
                                 ).then_inc(c_loaded, DMA)

                def load_mask(b):
                    sp.dma_start(mask_raw[:, :, :], mask[b].rearrange("(j p) k -> p j k", p=P)
                                 ).then_inc(mask_loaded, DMA)

                def load_res(b):
                    sp.dma_start(x_res[:, :, :], x_in[b].rearrange("(j p) d -> p j d", p=P)
                                 ).then_inc(res_loaded, DMA)

                def store(b):
                    sp.wait_ge(x_made, NT * b + NT)
                    sp.dma_start(x_out[b].rearrange("(j p) d -> p j d", p=P), x_res[:, :, :]
                                 ).then_inc(stored, DMA)

                def stack(half, b, first=False):
                    n_qk_lo_made = counted_to(sp, NQK * b + 4 * half + 4)
                    n_scored = counted_to(sp, PAIRS * (b - 1) + 4 * half + 4)
                    sp.wait_ge(ident_made, 1)
                    sp.wait_ge(qk_lo_made, n_qk_lo_made)
                    if not first:
                        sp.wait_ge(scored, n_scored)
                    for kind in range(2):
                        n = 2 * (2 * half + kind)
                        dst = (q_stack, k_stack)[kind]
                        blocks = ((qk_hi, qk_lo, qk_hi), (qk_hi, qk_hi, qk_lo))[kind]
                        for r, src in enumerate(blocks):
                            for i in range(HPG):
                                sp.dma_start(
                                    dst[HD * r:HD * r + HD, 8 * half + i:8 * half + 8:HPG, :].bitcast(F32),
                                    src[HD * i:HD * i + HD, n:n + 2, :].bitcast(F32)
                                ).then_inc(stacked[half], DMA)

                def weights(c):
                    if c >= 2:
                        sp.wait_ge(w_lo_made, c - 1)
                    src = w_qkv[:, c * H:c * H + H] if c < 3 else w_out
                    sp.dma_start(stage[c % 2], src.rearrange("(k p) n -> p k n", p=P)
                                 ).then_inc(w_loaded[c % 2], DMA)

                load_x(0)
                weights(0)
                weights(1)
                sp.dma_start(bqk[:, :], bias_qk).then_inc(consts_loaded, DMA)
                sp.dma_start(lns[:, :], ln_s).then_inc(consts_loaded, DMA)
                sp.dma_start(lnb[:, :], ln_b).then_inc(consts_loaded, DMA)
                sp.dma_start(bv_row[:, :], bias_v.broadcast_to([P, H])).then_inc(consts_loaded, DMA)
                sp.dma_start(bo_row[:, :], bias_o.broadcast_to([P, H])).then_inc(consts_loaded, DMA)
                load_mask(0)
                if cross:
                    load_c(0)
                weights(2)
                weights(3)
                sp.wait_ge(turned, 2)
                load_x(1)
                stack(0, 0, True)
                stack(1, 0, True)
                load_res(0)
                if cross:
                    sp.wait_ge(c_turned, 2)
                    load_c(1)
                    sp.wait_ge(mask_made, 1)
                    load_mask(1)

                def step(b, first=False, last=False, more=True):
                    if more and not last:
                        sp.wait_ge(turned, 2 * (b + 2))
                        load_x(b + 2)
                    if not first:
                        store(b - 1)
                        sp.wait_ge(stored, DMA * b)
                        load_res(b)
                    if not last:
                        stack(0, b + 1)
                        if cross and more:
                            sp.wait_ge(c_turned, 2 * (b + 2))
                            load_c(b + 2)
                        stack(1, b + 1)
                        if cross and more:
                            sp.wait_ge(mask_made, b + 2)
                            load_mask(b + 2)

                step(0, first=True)
                with sp.Fori(1, B - 2) as b:
                    step(b)
                step(B - 2, more=False)
                step(B - 1, last=True)
                store(B - 1)
                sp.wait_ge(stored, DMA * B)

            @block.gpsimd
            def _(pool):
                nc.gpsimd.memset(ident[:, :], 0.0).then_inc(ident_made, 1)
                nc.gpsimd.memset(neg_half[:, :], -0.5).then_inc(ident_made, 1)
                pool.wait_ge(ident_made, 2)
                nc.gpsimd.affine_select(out=ident[:, :], in_=ident[:, :], compare_op=ALU.not_equal,
                                        fill=1.0, base=0, pattern=[[-1, P]], channel_multiplier=1
                                        ).then_inc(ident_made, 1)

                def make_rstd(b):
                    n_mv_made = counted_to(pool, NT * b + NT)
                    n_z_made = counted_to(pool, NT * b)
                    pool.wait_ge(ident_made, 1)
                    pool.wait_ge(mv_made, n_mv_made)
                    if not isinstance(b, int) or b > 0:
                        pool.wait_ge(z_made, n_z_made)
                    nc.gpsimd.tensor_scalar(rstd[:, :], mean_var[:, :, 1], 1.0, EPS, ALU.mult, ALU.add
                                            ).then_inc(var_made, 1)
                    pool.wait_ge(var_made, b + 1)
                    nc.gpsimd.tensor_tensor(rstd[:, :], rstd[:, :], neg_half[:, :], ALU.pow
                                            ).then_inc(rstd_made, 1)

                def round_y(b, first=False):
                    n_y_made = counted_to(pool, KT * b + KT)
                    n_v_summed = counted_to(pool, NT * b)
                    pool.wait_ge(ident_made, 1)
                    pool.wait_ge(y_made, n_y_made)
                    if not first:
                        pool.wait_ge(v_summed, n_v_summed)
                    nc.gpsimd.tensor_scalar(y_hi[:, :, :], y[:, :, :], 1.0, 0.0, ALU.mult, ALU.add
                                            ).then_inc(y_hi_made, 1)

                def round_c(b, first=False):
                    n_c_copied = counted_to(pool, 2 * b + 2)
                    n_v_summed = counted_to(pool, NT * b)
                    pool.wait_ge(ident_made, 1)
                    pool.wait_ge(c_copied, n_c_copied)
                    if not first:
                        pool.wait_ge(v_summed, n_v_summed)
                    nc.gpsimd.tensor_scalar(c_hi[:, :, :], y[:, :, :], 1.0, 0.0, ALU.mult, ALU.add
                                            ).then_inc(c_hi_made, 1)

                def bias_res(b):
                    pool.wait_ge(res_loaded, DMA * b + DMA)
                    nc.gpsimd.tensor_tensor(x_res[:, :, :], x_res[:, :, :],
                                            bo_row[:, :].unsqueeze(1).to_broadcast([P, NT, H]),
                                            ALU.add).then_inc(res_biased, 1)

                def round_cx(b, first=False):
                    n_cx_made = counted_to(pool, GROUPS * b + GROUPS)
                    n_o_summed = counted_to(pool, NT * b)
                    pool.wait_ge(ident_made, 1)
                    pool.wait_ge(cx_made, n_cx_made)
                    if not first:
                        pool.wait_ge(o_summed, n_o_summed)
                    nc.gpsimd.tensor_scalar(cx_hi[:, :, :], cx[:, :, :], 1.0, 0.0, ALU.mult, ALU.add
                                            ).then_inc(cx_hi_made, 1)

                make_rstd(0)
                round_y(0, True)
                if cross:
                    round_c(0, True)
                make_rstd(1)
                pool.wait_ge(consts_loaded, DMA * NCONST)
                bias_res(0)

                def step(b, first=False, last=False, more=True):
                    if not last:
                        round_y(b + 1)
                        if cross:
                            round_c(b + 1)
                    if not first:
                        bias_res(b)
                    if more:
                        make_rstd(b + 2)
                    round_cx(b, first)

                step(0, first=True)
                with pool.Fori(1, B - 2) as b:
                    step(b)
                step(B - 2, more=False)
                step(B - 1, last=True, more=False)

            @block.scalar
            def _(act):
                def round_w(c):
                    act.wait_ge(w_loaded[c % 2], DMA * (c // 2 + 1))
                    dst = w_hi[:, :, c * H:c * H + H] if c < 3 else wo_hi[:, :, :]
                    nc.scalar.activation(dst, stage[c % 2], ACT.Copy).then_inc(w_hi_made, 1)

                def scale_y(b, first=False):
                    for k in range(KT):
                        if k % 2 == 0:
                            act.wait_ge(turned, 2 * b + k // 2 + 1)
                        if k == 0 and not first:
                            if cross:
                                act.wait_ge(c_lo_made, b)
                            else:
                                act.wait_ge(y_lo_made, b)
                        nc.scalar.activation(y[:, k, :], ps_p4[:, k, :], ACT.Identity,
                                             bias=lnb[:, k:k + 1], scale=lns[:, k:k + 1]
                                             ).then_inc(y_made, 1)

                def copy_c(b):
                    act.wait_ge(y_lo_made, b + 1)
                    for i in range(2):
                        act.wait_ge(c_turned, 2 * b + i + 1)
                        nc.scalar.activation(y[:, 2 * i:2 * i + 2, :], ps_p4[:, 2 * i:2 * i + 2, :],
                                             ACT.Copy).then_inc(c_copied, 1)

                def round_qk(b, c, first=False):
                    kind, tiles = CHUNKS[c]
                    for i, t in enumerate(tiles):
                        n = 2 * c + i
                        act.wait_ge(qk_summed, NQK * b + n + 1)
                        if i == 0 and c % 2 == 0 and not first:
                            act.wait_ge(stacked[c // 2], STACK_DMAS * DMA * b)
                        col = 4 * kind + t
                        nc.scalar.activation(qk_hi[:, n, :], ps_p[:, i, 0:S], ACT.Identity,
                                             bias=bqk[:, col:col + 1]).then_inc(qk_hi_made, 1)

                def exps(b, u, first=False):
                    if u % 2 == 0 and not (first and u < 4):
                        act.wait_ge(recip_made, GROUPS * b + u // 2 - 1)
                    for i in range(4):
                        h, t = i // 2, i % 2
                        act.wait_ge(masked, 4 * (PAIRS * b + u) + i + 1)
                        col = 2 * (u % 2) + h
                        nc.scalar.activation(sc[:, u % NS, h, t, :], sc[:, u % NS, h, t, :], ACT.Exp,
                                             bias=neg_max[:, u % NS, h, t:t + 1], scale=-1.0,
                                             accum_out=sums[:, (u // 2) % 2, t, col:col + 1]
                                             ).then_inc(exped, 1)

                def copy_probs(b, u, first=False):
                    g = u // 2
                    if u % 2 == 0 and not (first and g < 2):
                        act.wait_ge(pv_summed, GROUPS * b + g - 1)
                    act.wait_ge(probs_turned, 2 * (PAIRS * b + u) + 2)
                    nc.scalar.activation(probs_t[:, g % 2, 2 * (u % 2):2 * (u % 2) + 2, :, :],
                                         ps_t[:, :, :, :], ACT.Copy).then_inc(probs_made, 1)

                def copy_recip(b, g):
                    act.wait_ge(recip_turned, GROUPS * b + g + 1)
                    if not (isinstance(b, int) and b == 0 and g == 0):
                        act.wait_ge(cx_made, GROUPS * b + g)
                    nc.scalar.activation(recip_t[:, :], ps_r[:, 0:S], ACT.Copy).then_inc(recip_copied, 1)

                for c in range(WCHUNKS):
                    round_w(c)
                act.wait_ge(consts_loaded, DMA * NCONST)
                scale_y(0, True)
                if cross:
                    copy_c(0)
                for c in range(4):
                    round_qk(0, c, True)
                act.wait_ge(w_lo_made, WCHUNKS)

                def step(b, first=False, last=False):
                    for u in range(PAIRS):
                        exps(b, u, first)
                        if u >= 1:
                            copy_probs(b, u - 1, first)
                        if u == 0 and not last:
                            scale_y(b + 1)
                        if u == 2 and cross and not last:
                            copy_c(b + 1)
                        if u in QK_SLOTS and not last:
                            round_qk(b + 1, QK_SLOTS.index(u))
                        if u in (3, 5, 7):
                            copy_recip(b, (u - 3) // 2)
                    copy_probs(b, PAIRS - 1, first)
                    copy_recip(b, GROUPS - 1)

                step(0, first=True)
                with act.Fori(1, B - 1) as b:
                    step(b)
                step(B - 1, last=True)

            @block.vector
            def _(dve):
                def split_w(c):
                    dve.wait_ge(w_hi_made, c + 1)
                    hi = w_hi[:, :, c * H:c * H + H] if c < 3 else wo_hi[:, :, :]
                    lo = w_lo[:, :, c * H:c * H + H] if c < 3 else wo_lo[:, :, :]
                    nc.vector.tensor_tensor(lo, stage[c % 2], hi.bitcast(F32), ALU.subtract
                                            ).then_inc(w_lo_made, 1)

                def norm_stats(b):
                    dve.wait_ge(x_loaded, DMA * b + DMA)
                    for j in range(NT):
                        nc.vector.bn_stats(stats[:, j, :], x_ln[:, j, :]).then_inc(stats_made, 1)
                    for j in range(NT):
                        n_stats_made = counted_to(dve, NT * b + j + 1)
                        dve.wait_ge(ident_made, 1)
                        dve.wait_ge(stats_made, n_stats_made)
                        nc.vector.bn_aggr(mean_var[:, j, :], stats[:, j, :]).then_inc(mv_made, 1)

                def normalise(b):
                    dve.wait_ge(rstd_made, b + 1)
                    for j in range(NT):
                        nc.vector.tensor_scalar(x_ln[:, j, :], x_ln[:, j, :], mean_var[:, j, 0:1],
                                                rstd[:, j:j + 1], ALU.subtract, ALU.mult
                                                ).then_inc(z_made, 1)

                def split_y(b):
                    dve.wait_ge(y_hi_made, b + 1)
                    nc.vector.tensor_tensor(y_lo[:, :, :], y[:, :, :], y_hi[:, :, :].bitcast(F32),
                                            ALU.subtract).then_inc(y_lo_made, 1)

                def split_c(b):
                    dve.wait_ge(c_hi_made, b + 1)
                    nc.vector.tensor_tensor(c_lo[:, :, :], y[:, :, :], c_hi[:, :, :].bitcast(F32),
                                            ALU.subtract).then_inc(c_lo_made, 1)

                def split_qk(b, c):
                    kind, tiles = CHUNKS[c]
                    for i, t in enumerate(tiles):
                        n = 2 * c + i
                        dve.wait_ge(qk_hi_made, NQK * b + n + 1)
                        col = 4 * kind + t
                        nc.vector.scalar_tensor_tensor(
                            out=qk_lo[:, n, :], in0=ps_p[:, i, 0:S], scalar=bqk[:, col:col + 1],
                            in1=qk_hi[:, n, :].bitcast(F32), op0=ALU.add, op1=ALU.subtract
                        ).then_inc(qk_lo_made, 1)

                def bias_v_rows(b, first=False):
                    if not first:
                        dve.wait_ge(pv_summed, GROUPS * b)
                    for j in range(NT):
                        dve.wait_ge(v_summed, NT * b + j + 1)
                        nc.vector.tensor_tensor(v[:, j, :], ps_p[:, j, :], bv_row[:, :], ALU.add
                                                ).then_inc(v_made, 1)

                def make_mask(b):
                    dve.wait_ge(mask_loaded, DMA * b + DMA)
                    if not (isinstance(b, int) and b == 0):
                        dve.wait_ge(masked, 4 * PAIRS * b)
                    nc.vector.tensor_scalar(mask_mul[:, :, :], mask_raw[:, :, :], HD ** -0.5, None,
                                            ALU.mult).then_inc(mask_mul_made, 1)
                    nc.vector.tensor_scalar(mask_add[:, :, :], mask_raw[:, :, :], 10000.0, -10000.0,
                                            ALU.mult, ALU.add).then_inc(mask_made, 1)

                def mask_scores(b, u, first=False):
                    if u == 0 and (first or cross):
                        dve.wait_ge(mask_made, b + 1)
                    dve.wait_ge(scored, PAIRS * b + u + 1)
                    if not (first and u < NS):
                        dve.wait_ge(probs_turned, 2 * (PAIRS * b + u - NS + 1))
                    s = u % NS
                    nc.vector.tensor_tensor(
                        sc[:, s, :, :, :].rearrange("p h t k -> p h (t k)"),
                        ps_s[:, :, :, :].rearrange("p h t k -> p h (t k)"),
                        mask_mul[:, :, :].rearrange("p t k -> p (t k)").unsqueeze(1)
                        .to_broadcast([P, 2, NT * S]), ALU.mult).then_inc(multiplied, 1)
                    n_multiplied = counted_to(dve, PAIRS * b + u + 1)
                    dve.wait_ge(ident_made, 1)
                    dve.wait_ge(multiplied, n_multiplied)
                    for i in range(4):
                        h, t = i // 2, i % 2
                        nc.vector.tensor_tensor_reduce(
                            out=sc[:, s, h, t, :], in0=sc[:, s, h, t, :], in1=mask_add[:, t, :],
                            scale=-1.0, scalar=3e38, op0=ALU.add, op1=ALU.min,
                            accum_out=neg_max[:, s, h, t:t + 1]).then_inc(masked, 1)

                def recips(b, g):
                    dve.wait_ge(exped, 4 * (PAIRS * b + 2 * g + 2))
                    nc.vector.reciprocal(recip[:, g % 2, :, :], sums[:, g % 2, :, :]).then_inc(recip_made, 1)
                    dve.wait_ge(recip_made, GROUPS * b + g + 1)
                    if not (isinstance(b, int) and b == 0 and g == 0):
                        dve.wait_ge(recip_turned, GROUPS * b + g)
                    nc.vector.tensor_copy(recip_b[:, :, :, :].rearrange("p t h d -> p (t h) d"),
                                          recip[:, g % 2, :, :].rearrange("p t h -> p (t h)")
                                          .unsqueeze(2).to_broadcast([P, NT * HPG, HD])
                                          ).then_inc(recip_spread, 1)

                def scale_cx(b, g, first=False):
                    if g == 0 and not first:
                        dve.wait_ge(cx_lo_made, b)
                    dve.wait_ge(pv_summed, GROUPS * b + g + 1)
                    dve.wait_ge(recip_copied, GROUPS * b + g + 1)
                    nc.vector.tensor_tensor(cx[:, g, :], ps_c[:, 0:S], recip_t[:, :], ALU.mult
                                            ).then_inc(cx_made, 1)

                def split_cx(b):
                    dve.wait_ge(cx_hi_made, b + 1)
                    nc.vector.tensor_tensor(cx_lo[:, :, :], cx[:, :, :], cx_hi[:, :, :].bitcast(F32),
                                            ALU.subtract).then_inc(cx_lo_made, 1)

                def add_res(b):
                    dve.wait_ge(res_biased, b + 1)
                    for j in range(NT):
                        dve.wait_ge(o_summed, NT * b + j + 1)
                        nc.vector.tensor_tensor(x_res[:, j, :], ps_p[:, j, :], x_res[:, j, :], ALU.add
                                                ).then_inc(x_made, 1)

                norm_stats(0)
                normalise(0)
                for c in range(WCHUNKS):
                    split_w(c)
                split_y(0)
                if cross:
                    split_c(0)
                for c in range(4):
                    split_qk(0, c)
                dve.wait_ge(consts_loaded, DMA * NCONST)
                bias_v_rows(0, True)
                make_mask(0)
                norm_stats(1)
                normalise(1)

                def step(b, first=False, last=False, more=True):
                    for u in range(PAIRS):
                        mask_scores(b, u, first)
                        if u == 0 and not last:
                            split_y(b + 1)
                        if u == 1 and not first:
                            add_res(b - 1)
                        if u == 2 and cross and not last:
                            split_c(b + 1)
                        if u in QK_SLOTS and not last:
                            split_qk(b + 1, QK_SLOTS.index(u))
                        if u in (2, 4, 6):
                            recips(b, (u - 2) // 2)
                        if u in (3, 5, 7):
                            scale_cx(b, (u - 3) // 2, first)
                    if cross and not last:
                        make_mask(b + 1)
                    recips(b, GROUPS - 1)
                    if more:
                        norm_stats(b + 2)
                    scale_cx(b, GROUPS - 1, first)
                    if not last:
                        bias_v_rows(b + 1)
                    if more:
                        normalise(b + 2)
                    split_cx(b)

                step(0, first=True)
                with dve.Fori(1, B - 2) as b:
                    step(b)
                step(B - 2, more=False)
                step(B - 1, last=True, more=False)
                add_res(B - 1)

            @block.tensor
            def _(pe):
                def passes(out, lhs, rhs, l_slice, r_slice, steps, done):
                    n = 0
                    for k in range(steps):
                        for a, w in ((0, 0), (1, 0), (0, 1)):
                            ins = nc.tensor.matmul(out, l_slice(lhs[a], k), r_slice(rhs[w], k),
                                                   start=(n == 0), stop=(n == 3 * steps - 1))
                            n += 1
                    ins.then_inc(done, 1)

                def turn(src, done):
                    for i in range(2):
                        for k in (2 * i, 2 * i + 1):
                            for j in range(NT):
                                ins = nc.tensor.transpose(ps_p4[:, k, j * P:j * P + P],
                                                          src[:, j, k * P:k * P + P], ident[:, :])
                        ins.then_inc(done, 1)

                def turn_x(b, first=False):
                    if first:
                        pe.wait_ge(ident_made, 3)
                    else:
                        pe.wait_ge(v_made, NT * b)
                    pe.wait_ge(z_made, NT * b + NT)
                    turn(x_ln, turned)

                def turn_c(b, after_o=None):
                    pe.wait_ge(c_loaded, DMA * b + DMA)
                    pe.wait_ge(y_made, KT * b + KT)
                    if after_o is not None:
                        pe.wait_ge(x_made, NT * after_o + NT)
                    turn(c_nat, c_turned)

                def project_qk(b, c, after_o=None):
                    kind, tiles = CHUNKS[c]
                    src = (c_hi, c_lo) if cross and kind else (y_hi, y_lo)
                    if c == 0:
                        pe.wait_ge(y_lo_made, b + 1)
                        if after_o is not None:
                            pe.wait_ge(x_made, NT * after_o + NT)
                        if cross:
                            pe.wait_ge(c_copied, 2 * b + 2)
                    if c == 1 and cross:
                        pe.wait_ge(c_lo_made, b + 1)
                    for i, t in enumerate(tiles):
                        if c > 0:
                            pe.wait_ge(qk_lo_made, NQK * b + 2 * c - 1 + i)
                        col = (4 * kind + t) * P
                        passes(ps_p[:, i, 0:S], (w_hi, w_lo), src, lambda w, k: w[:, k, col:col + P],
                               lambda a, k: a[:, k, :], KT, qk_summed)

                def project_v(b):
                    src = (c_hi, c_lo) if cross else (y_hi, y_lo)
                    for j in range(NT):
                        pe.wait_ge(qk_lo_made, NQK * b + NQK - 1 + j)
                        passes(ps_p[:, j, :], src, (w_hi, w_lo), lambda a, k: a[:, k, j * P:j * P + P],
                               lambda w, k: w[:, k, 2 * H:3 * H], KT, v_summed)

                def project_o(b):
                    pe.wait_ge(cx_lo_made, b + 1)
                    for j in range(NT):
                        passes(ps_p[:, j, :], (cx_hi, cx_lo), (wo_hi, wo_lo),
                               lambda a, k: a[:, k, j * P:j * P + P], lambda w, k: w[:, k, :],
                               KT, o_summed)

                def scores(b, u, first=False):
                    if u % 4 == 0:
                        pe.wait_ge(stacked[u // 4], STACK_DMAS * DMA * (b + 1))
                    if not (first and u == 0):
                        pe.wait_ge(multiplied, PAIRS * b + u)
                    for h in range(2):
                        for t in range(NT):
                            ins = nc.tensor.matmul(ps_s[:, h, t, :],
                                                   q_stack[0:3 * HD, 2 * u + h, t * P:t * P + P],
                                                   k_stack[0:3 * HD, 2 * u + h, :], start=True, stop=True)
                    ins.then_inc(scored, 1)

                def turn_probs(b, u, first=False):
                    pe.wait_ge(exped, 4 * (PAIRS * b + u) + 4)
                    if not (first and u == 0):
                        pe.wait_ge(probs_made, PAIRS * b + u)
                    for h in range(2):
                        for k in range(NT):
                            for t in range(NT):
                                ins = nc.tensor.transpose(ps_t[:, h, k, t * P:t * P + P],
                                                          sc[:, u % NS, h, t, k * P:k * P + P],
                                                          ident[:, :])
                        ins.then_inc(probs_turned, 1)

                def weigh_v(b, g, first=False):
                    pe.wait_ge(recip_spread, GROUPS * b + g + 1)
                    if not (first and g == 0):
                        pe.wait_ge(recip_copied, GROUPS * b + g)
                    for t in range(NT):
                        ins = nc.tensor.transpose(ps_r[:, t * P:t * P + P],
                                                  recip_b[:, t, :, :].rearrange("p h d -> p (h d)"),
                                                  ident[:, :])
                    ins.then_inc(recip_turned, 1)
                    pe.wait_ge(probs_made, PAIRS * b + 2 * g + 2)
                    if g == 0:
                        pe.wait_ge(v_made, NT * b + NT)
                    if not (first and g == 0):
                        pe.wait_ge(cx_made, GROUPS * b + g)
                    for k in range(NT):
                        for h in range(HPG):
                            ins = nc.tensor.matmul(
                                ps_c[HD * h:HD * h + HD, 0:S],
                                v[:, k, (HPG * g + h) * HD:(HPG * g + h) * HD + HD],
                                probs_t[:, g % 2, h, k, :], start=(k == 0), stop=(k == NT - 1))
                    ins.then_inc(pv_summed, 1)

                turn_x(0, True)
                if cross:
                    turn_c(0)
                pe.wait_ge(w_lo_made, WCHUNKS)
                for c in range(4):
                    project_qk(0, c)
                project_v(0)

                def step(b, first=False, last=False):
                    for u in range(PAIRS):
                        scores(b, u, first)
                        if u in (3, 5, 7):
                            weigh_v(b, (u - 3) // 2, first)
                        if u >= 1:
                            turn_probs(b, u - 1, first)
                        if u == 0 and not last:
                            turn_x(b + 1)
                        if u == 1 and not first:
                            if last:
                                pe.wait_ge(v_made, NT * b + NT)
                            else:
                                pe.wait_ge(y_made, KT * b + 2 * KT)
                            project_o(b - 1)
                        if u == 2 and cross and not last:
                            turn_c(b + 1, None if first else b - 1)
                        if u in QK_SLOTS and not last:
                            project_qk(b + 1, QK_SLOTS.index(u), None if first or cross else b - 1)
                    turn_probs(b, PAIRS - 1, first)
                    weigh_v(b, GROUPS - 1, first)
                    if not last:
                        project_v(b + 1)

                step(0, first=True)
                with pe.Fori(1, B - 1) as b:
                    step(b)
                step(B - 1, last=True)
                pe.wait_ge(x_made, NT * (B - 1))
                project_o(B - 1)

        nc.clear_and_free_semaphores(sems)
        nc.all_engine_barrier()


def mlp_phase(nc, x_in, x_out, w1, w2, b1, b2, ln_s, ln_b):
    name = "mlp"
    MT = F // P
    M = MT // 2
    LAG = 2
    RING = 4
    NCONST = 4
    with ExitStack() as ctx:
        sems = []

        def sb(n, shape, dtype=F32):
            return ctx.enter_context(nc.sbuf_tensor(f"{name}_{n}", shape, dtype))

        def pb(n, shape):
            return ctx.enter_context(nc.psum_tensor(f"{name}_{n}", shape, F32))

        def sem(n):
            sems.append(nc.alloc_semaphore(f"{name}_{n}"))
            return sems[-1]

        w1_hi = sb("w1_hi", [P, KT, F], F32R)
        w1_lo = sb("w1_lo", [P, KT, F], F32R)
        w2_hi = sb("w2_hi", [P, MT, H], F32R)
        w2_lo = sb("w2_lo", [P, MT, H], F32R)
        stage = sb("stage", [P, 2, KT, H])
        b1_col = sb("b1_col", [P, MT])
        b2_row = sb("b2_row", [P, H])
        lns = sb("lns", [P, KT])
        lnb = sb("lnb", [P, KT])
        ident = sb("ident", [P, P])
        neg_half = sb("neg_half", [P, NT])
        x_ln = sb("x_ln", [P, NT, H])
        x_res = sb("x_res", [P, NT, H])
        stats = sb("stats", [P, NT, 6])
        mean_var = sb("mean_var", [P, NT, 2])
        rstd = sb("rstd", [P, NT])
        y = sb("y", [P, KT, S])
        y_hi = sb("y_hi", [P, 2, KT, S], F32R)
        y_lo = sb("y_lo", [P, 2, KT, S], F32R)
        g = sb("g", [P, 2, 2, S])
        g_hi = sb("g_hi", [P, RING, 2, S], F32R)
        g_lo = sb("g_lo", [P, RING, 2, S], F32R)

        ps_h = pb("ps_h", [P, 2, 2, S])
        ps_o = pb("ps_o", [P, 2, NT, H])
        ps_x = pb("ps_x", [P, KT, S])

        consts_loaded, ident_made = sem("consts_loaded"), sem("ident_made")
        w_loaded = [sem(f"w_loaded{i}") for i in range(2)]
        w_hi_made, w_lo_made = sem("w_hi_made"), sem("w_lo_made")
        x_loaded, res_loaded, stored = sem("x_loaded"), sem("res_loaded"), sem("stored")
        stats_made, mv_made = sem("stats_made"), sem("mv_made")
        var_made, rstd_made = sem("var_made"), sem("rstd_made")
        z_made, turned, y_made = sem("z_made"), sem("turned"), sem("y_made")
        y_hi_made, y_lo_made = sem("y_hi_made"), sem("y_lo_made")
        h_summed, g_made = sem("h_summed"), sem("g_made")
        g_hi_made, g_lo_made = sem("g_hi_made"), sem("g_lo_made")
        o_added, res_biased, x_made = sem("o_added"), sem("res_biased"), sem("x_made")

        WCHUNKS = 8

        def w_dst(w1_part, w2_part, c):
            return w1_part[:, :, c * H:c * H + H] if c < 4 else w2_part[:, 4 * (c - 4):4 * (c - 4) + 4, :]

        with nc.Block() as block:

            @block.sync
            def _(sp):
                def load_x(b):
                    sp.dma_start(x_ln[:, :, :], x_in[b].rearrange("(j p) d -> p j d", p=P)
                                 ).then_inc(x_loaded, DMA)

                def load_res(b):
                    sp.dma_start(x_res[:, :, :], x_in[b].rearrange("(j p) d -> p j d", p=P)
                                 ).then_inc(res_loaded, DMA)

                def store(b):
                    sp.wait_ge(x_made, NT * b + NT)
                    sp.dma_start(x_out[b].rearrange("(j p) d -> p j d", p=P), x_res[:, :, :]
                                 ).then_inc(stored, DMA)

                load_x(0)
                for c in range(WCHUNKS):
                    if c >= 2:
                        sp.wait_ge(w_lo_made, c - 1)
                    src = w1[:, c * H:c * H + H] if c < 4 else w2[(c - 4) * H:(c - 3) * H, :]
                    sp.dma_start(stage[:, c % 2, :, :], src.rearrange("(k p) n -> p k n", p=P)
                                 ).then_inc(w_loaded[c % 2], DMA)
                    if c == 1:
                        sp.dma_start(lns[:, :], ln_s).then_inc(consts_loaded, DMA)
                        sp.dma_start(lnb[:, :], ln_b).then_inc(consts_loaded, DMA)
                        sp.dma_start(b1_col[:, :], b1).then_inc(consts_loaded, DMA)
                        sp.dma_start(b2_row[:, :], b2.broadcast_to([P, H])).then_inc(consts_loaded, DMA)
                load_res(0)
                sp.wait_ge(turned, 2)
                load_x(1)

                def step(b, first=False, last=False):
                    if not first:
                        store(b - 1)
                        sp.wait_ge(stored, DMA * b)
                        load_res(b)
                    if not last:
                        sp.wait_ge(turned, 2 * (b + 2))
                        load_x(b + 2)

                step(0, first=True)
                with sp.Fori(1, B - 2) as b:
                    step(b)
                step(B - 2, last=True)
                step(B - 1, last=True)
                store(B - 1)
                sp.wait_ge(stored, DMA * B)

            @block.gpsimd
            def _(pool):
                nc.gpsimd.memset(ident[:, :], 0.0).then_inc(ident_made, 1)
                nc.gpsimd.memset(neg_half[:, :], -0.5).then_inc(ident_made, 1)
                pool.wait_ge(ident_made, 2)
                nc.gpsimd.affine_select(out=ident[:, :], in_=ident[:, :], compare_op=ALU.not_equal,
                                        fill=1.0, base=0, pattern=[[-1, P]], channel_multiplier=1
                                        ).then_inc(ident_made, 1)

                def make_rstd(b, first=False):
                    n_mv_made = counted_to(pool, NT * b + NT)
                    n_z_made = counted_to(pool, NT * b)
                    pool.wait_ge(ident_made, 1)
                    pool.wait_ge(mv_made, n_mv_made)
                    if not first:
                        pool.wait_ge(z_made, n_z_made)
                    nc.gpsimd.tensor_scalar(rstd[:, :], mean_var[:, :, 1], 1.0, EPS, ALU.mult, ALU.add
                                            ).then_inc(var_made, 1)
                    pool.wait_ge(var_made, b + 1)
                    nc.gpsimd.tensor_tensor(rstd[:, :], rstd[:, :], neg_half[:, :], ALU.pow
                                            ).then_inc(rstd_made, 1)

                def round_y(b, par, early=False):
                    n_y_made = counted_to(pool, KT * b + KT)
                    n_h_summed = counted_to(pool, M * (b - 1))
                    pool.wait_ge(ident_made, 1)
                    pool.wait_ge(y_made, n_y_made)
                    if not early:
                        pool.wait_ge(h_summed, n_h_summed)
                    nc.gpsimd.tensor_scalar(y_hi[:, par, :, :], y[:, :, :], 1.0, 0.0, ALU.mult, ALU.add
                                            ).then_inc(y_hi_made, 1)

                def round_g(b, m, first=False):
                    n_g_made = counted_to(pool, 2 * (M * b + m) + 2)
                    n_o_added = counted_to(pool, M * b + m - RING + 1)
                    pool.wait_ge(ident_made, 1)
                    pool.wait_ge(g_made, n_g_made)
                    if not (first and m < RING):
                        pool.wait_ge(o_added, n_o_added)
                    nc.gpsimd.tensor_scalar(g_hi[:, m % RING, :, :], g[:, m % 2, :, :], 1.0, 0.0,
                                            ALU.mult, ALU.add).then_inc(g_hi_made, 1)

                make_rstd(0, True)
                round_y(0, 0, True)

                def step(b, par, first=False, last=False):
                    for m in range(M):
                        round_g(b, m, first)
                        if m == 2:
                            pool.wait_ge(res_loaded, DMA * b + DMA)
                            if first:
                                pool.wait_ge(consts_loaded, DMA * NCONST)
                            nc.gpsimd.tensor_tensor(x_res[:, :, :], x_res[:, :, :],
                                                    b2_row[:, :].unsqueeze(1).to_broadcast([P, NT, H]),
                                                    ALU.add).then_inc(res_biased, 1)
                        if m == 3 and not last:
                            make_rstd(b + 1)
                        if m == 6 and not last:
                            round_y(b + 1, 1 - par, first)

                step(0, 0, first=True)
                with pool.Fori(0, (B - 2) // 2) as i:
                    step(2 * i + 1, 1)
                    step(2 * i + 2, 0)
                step(B - 1, 1, last=True)

            @block.scalar
            def _(act):
                def round_w(c):
                    act.wait_ge(w_loaded[c % 2], DMA * (c // 2 + 1))
                    nc.scalar.activation(w_dst(w1_hi, w2_hi, c), stage[:, c % 2, :, :], ACT.Copy
                                         ).then_inc(w_hi_made, 1)

                def scale_y(b, first=False):
                    for k in range(KT):
                        if k % 2 == 0:
                            act.wait_ge(turned, 2 * b + k // 2 + 1)
                        if k == 0 and not first:
                            act.wait_ge(y_lo_made, b)
                        nc.scalar.activation(y[:, k, :], ps_x[:, k, :], ACT.Identity,
                                             bias=lnb[:, k:k + 1], scale=lns[:, k:k + 1]
                                             ).then_inc(y_made, 1)

                def gelus(b, m, first=False):
                    act.wait_ge(h_summed, M * b + m + 1)
                    if not (first and m < 2):
                        act.wait_ge(g_lo_made, M * b + m - 1)
                    for i in range(2):
                        nc.scalar.activation(g[:, m % 2, i, :], ps_h[:, m % 2, i, :],
                                             ACT.Gelu_apprx_tanh, bias=b1_col[:, 2 * m + i:2 * m + i + 1]
                                             ).then_inc(g_made, 1)

                act.wait_ge(consts_loaded, DMA * NCONST)
                scale_y(0, True)
                for c in range(4):
                    round_w(c)

                def step(b, first=False, last=False):
                    for m in range(M):
                        gelus(b, m, first)
                        if first and m < 4:
                            round_w(4 + m)
                        if m == 5 and not last:
                            scale_y(b + 1)

                step(0, first=True)
                with act.Fori(1, B - 1) as b:
                    step(b)
                step(B - 1, last=True)

            @block.vector
            def _(dve):
                def split_w(c):
                    dve.wait_ge(w_hi_made, c + 1)
                    nc.vector.tensor_tensor(w_dst(w1_lo, w2_lo, c), stage[:, c % 2, :, :],
                                            w_dst(w1_hi, w2_hi, c).bitcast(F32), ALU.subtract
                                            ).then_inc(w_lo_made, 1)

                def norm_stats(b):
                    dve.wait_ge(x_loaded, DMA * b + DMA)
                    for j in range(NT):
                        nc.vector.bn_stats(stats[:, j, :], x_ln[:, j, :]).then_inc(stats_made, 1)
                    for j in range(NT):
                        n_stats_made = counted_to(dve, NT * b + j + 1)
                        dve.wait_ge(ident_made, 1)
                        dve.wait_ge(stats_made, n_stats_made)
                        nc.vector.bn_aggr(mean_var[:, j, :], stats[:, j, :]).then_inc(mv_made, 1)

                def normalise(b):
                    dve.wait_ge(rstd_made, b + 1)
                    for j in range(NT):
                        nc.vector.tensor_scalar(x_ln[:, j, :], x_ln[:, j, :], mean_var[:, j, 0:1],
                                                rstd[:, j:j + 1], ALU.subtract, ALU.mult
                                                ).then_inc(z_made, 1)

                def split_y(b, par):
                    dve.wait_ge(y_hi_made, b + 1)
                    nc.vector.tensor_tensor(y_lo[:, par, :, :], y[:, :, :],
                                            y_hi[:, par, :, :].bitcast(F32), ALU.subtract
                                            ).then_inc(y_lo_made, 1)

                def split_g(b, m):
                    dve.wait_ge(g_hi_made, M * b + m + 1)
                    nc.vector.tensor_tensor(g_lo[:, m % RING, :, :], g[:, m % 2, :, :],
                                            g_hi[:, m % RING, :, :].bitcast(F32), ALU.subtract
                                            ).then_inc(g_lo_made, 1)

                def add_res(b, par):
                    dve.wait_ge(res_biased, b + 1)
                    dve.wait_ge(o_added, M * b + M)
                    for j in range(NT):
                        nc.vector.tensor_tensor(x_res[:, j, :], ps_o[:, par, j, :], x_res[:, j, :],
                                                ALU.add).then_inc(x_made, 1)

                norm_stats(0)
                normalise(0)
                for c in range(4):
                    split_w(c)
                split_y(0, 0)

                def step(b, par, first=False, last=False):
                    for m in range(M):
                        split_g(b, m)
                        if first and m < 4:
                            split_w(4 + m)
                        if m == 1 and not first:
                            add_res(b - 1, 1 - par)
                        if m == 2 and not last:
                            norm_stats(b + 1)
                        if m == 4 and not last:
                            normalise(b + 1)
                        if m == 6 and not last:
                            split_y(b + 1, 1 - par)

                step(0, 0, first=True)
                with dve.Fori(0, (B - 2) // 2) as i:
                    step(2 * i + 1, 1)
                    step(2 * i + 2, 0)
                step(B - 1, 1, last=True)
                add_res(B - 1, 1)

            @block.tensor
            def _(pe):
                def turn_x(b):
                    pe.wait_ge(z_made, NT * b + NT)
                    for i in range(2):
                        for k in (2 * i, 2 * i + 1):
                            for j in range(NT):
                                ins = nc.tensor.transpose(ps_x[:, k, j * P:j * P + P],
                                                          x_ln[:, j, k * P:k * P + P], ident[:, :])
                        ins.then_inc(turned, 1)

                def hidden(b, m, par, first=False):
                    if m == 0:
                        pe.wait_ge(y_lo_made, b + 1)
                    if not (first and m < 2):
                        pe.wait_ge(g_made, 2 * (M * b + m - 1))
                    for i in range(2):
                        col = (2 * m + i) * P
                        n = 0
                        for k in range(KT):
                            for w, a in ((w1_hi, y_hi), (w1_lo, y_hi), (w1_hi, y_lo)):
                                ins = nc.tensor.matmul(ps_h[:, m % 2, i, :], w[:, k, col:col + P],
                                                       a[:, par, k, :], start=(n == 0),
                                                       stop=(n == 3 * KT - 1))
                                n += 1
                    ins.then_inc(h_summed, 1)

                def output(b, m, par, first=False):
                    pe.wait_ge(g_lo_made, M * b + m + 1)
                    if m == 0 and not first:
                        pe.wait_ge(x_made, NT * (b - 1))
                    for j in range(NT):
                        n = 0
                        for i in range(2):
                            for a, w in ((g_hi, w2_hi), (g_lo, w2_hi), (g_hi, w2_lo)):
                                ins = nc.tensor.matmul(ps_o[:, par, j, :],
                                                       a[:, m % RING, i, j * P:j * P + P],
                                                       w[:, 2 * m + i, :], start=(m == 0 and n == 0),
                                                       stop=(m == M - 1 and n == 5))
                                n += 1
                    ins.then_inc(o_added, 1)

                pe.wait_ge(ident_made, 3)
                turn_x(0)
                pe.wait_ge(w_lo_made, 4)

                def step(b, par, first=False, second=False, last=False):
                    for m in range(M):
                        hidden(b, m, par, first)
                        if m >= LAG:
                            if first and m % 2 == 0:
                                pe.wait_ge(w_lo_made, 4 + m // 2)
                            output(b, m - LAG, par, first or second)
                        elif not first:
                            output(b - 1, m + M - LAG, 1 - par)
                        if m == 4 and not last:
                            pe.wait_ge(y_made, KT * b + KT)
                            turn_x(b + 1)

                step(0, 0, first=True)
                pe.wait_ge(w_lo_made, WCHUNKS)
                step(1, 1, second=True)
                with pe.Fori(1, (B - 2) // 2) as i:
                    step(2 * i, 0)
                    step(2 * i + 1, 1)
                step(B - 2, 0)
                step(B - 1, 1, last=True)
                for m in range(M - LAG, M):
                    output(B - 1, m, 1)

        nc.clear_and_free_semaphores(sems)
        nc.all_engine_barrier()


def style_phase(nc, x_in, context, keep, out, wq, wk, wv, bq, bk, bv):
    name = "style"
    C, T = S, H
    CT = C // P
    TB = T // P
    D = C // NH
    HT = P // D
    ROW_MASK, ROW_MAX = 3 * D, 3 * D + 1
    NB = NH // 2
    GROUPS = NH // 4
    HG = 2 * GROUPS
    SCALE = D ** -0.5
    BIG = 1e30
    NCONST = 3
    STACK_DMAS = 2 * 3 * HT + 2
    ROW_DMAS = HT
    OUT_DMAS = 8
    with ExitStack() as ctx:
        sems = []

        def sb(n, shape, dtype=F32):
            return ctx.enter_context(nc.sbuf_tensor(f"{name}_{n}", shape, dtype))

        def pb(n, shape):
            return ctx.enter_context(nc.psum_tensor(f"{name}_{n}", shape, F32))

        def sem(n):
            sems.append(nc.alloc_semaphore(f"{name}_{n}"))
            return sems[-1]

        w_nat = sb("w_nat", [P, 3, CT, C])
        w_hi = sb("w_hi", [P, 3, CT, C], F32R)
        w_lo = sb("w_lo", [P, 3, CT, C], F32R)
        b_col = sb("b_col", [P, 2, CT])
        bv_row = sb("bv_row", [P, C])
        ident = sb("ident", [P, P])
        minus_odd = sb("minus_odd", [2 * HT, 1])
        ones = sb("ones", [P, 2 * D])
        neg_half = sb("neg_half", [P, CT])
        xc = sb("xc", [P, 2, CT, T])
        xc_hi = sb("xc_hi", [P, 2, CT, T], F32R)
        xc_lo = sb("xc_lo", [P, 2, CT, T], F32R)
        qk_hi = sb("qk_hi", [P, 2 * CT, T], F32R)
        qk_lo = sb("qk_lo", [P, 2 * CT, T], F32R)
        q_stack = [sb(f"q_stack{i}", [P, NB, T], F32R) for i in range(2)]
        k_stack = [sb(f"k_stack{i}", [P, NB, T], F32R) for i in range(2)]
        vv = sb("vv", [P, 2, TB, NH, 2 * D])
        keep_u8 = sb("keep_u8", [1, T], U8)
        key_row = sb("key_row", [1, T], F32R)
        mx = sb("mx", [P, TB, HT])
        mx2 = sb("mx2", [P, TB, 2 * HT])
        max_hi = sb("max_hi", [2 * HT, T], F32R)
        max_row = sb("max_row", [2 * HT, T], F32R)
        probs = sb("probs", [P, 2, 4, 2, T])
        rough = sb("rough", [P, T])
        newton = sb("newton", [P, T])
        moments = sb("moments", [P, 2, T])
        mean = sb("mean", [P, CT, T])
        second = sb("second", [P, CT, T])
        xf = sb("xf", [P, CT, T])
        work = sb("work", [P, CT, T])
        keep_b8 = sb("keep_b8", [P, T], U8)
        keep_b = sb("keep_b", [P, T])
        junk = sb("junk", [P, T])
        sum_x = sb("sum_x", [P, CT])
        sum_xx = sb("sum_xx", [P, CT])
        count = sb("count", [P, 1])
        small = sb("small", [P, 6, CT])
        MEAN, SEC, SQ, VAR, RSTD, RCNT = range(6)

        ps_a = pb("ps_a", [P, 2, T])
        ps_s = pb("ps_s", [P, 2, 2, T])
        ps_m = pb("ps_m", [P, T])
        ps_d = pb("ps_d", [P, T])

        (consts_loaded, weights_loaded, w_hi_made, w_lo_made, ident_made, odd_made, ones_made,
         stacks_set) = (sem(n) for n in ("consts_loaded", "weights_loaded", "w_hi_made", "w_lo_made",
                                         "ident_made", "odd_made", "ones_made", "stacks_set"))
        xc_loaded, xc_hi_made, xc_lo_made = sem("xc_loaded"), sem("xc_hi_made"), sem("xc_lo_made")
        qk_summed, qk_hi_made, qk_lo_made = sem("qk_summed"), sem("qk_hi_made"), sem("qk_lo_made")
        keep_loaded, key_made = sem("keep_loaded"), sem("key_made")
        stacked = [sem(f"stacked{i}") for i in range(2)]
        v_summed, v_made, vv_made = sem("v_summed"), sem("v_made"), sem("vv_made")
        scored, maxed, mx2_made = sem("scored"), sem("maxed"), sem("mx2_made")
        max_turned, max_hi_made, max_made = sem("max_turned"), sem("max_hi_made"), sem("max_made")
        max_placed = [sem(f"max_placed{i}") for i in range(2)]
        rescored, exped = sem("rescored"), sem("exped")
        weighed, log_made, rough_made = sem("weighed"), sem("log_made"), sem("rough_made")
        newton_made, refined, moments_made = sem("newton_made"), sem("refined"), sem("moments_made")
        moments_moved = [sem(f"moments_moved{i}") for i in range(2)]
        xf_loaded, keep_b_loaded, keep_b_made = sem("xf_loaded"), sem("keep_b_loaded"), sem("keep_b_made")
        x_kept, summed, counted = sem("x_kept"), sem("summed"), sem("counted")
        count_made = sem("count_made")
        small_made, rstd_made, x_normed = sem("small_made"), sem("rstd_made"), sem("x_normed")
        squared, var_made, clipped, rooted = sem("squared"), sem("var_made"), sem("clipped"), sem("rooted")
        styled, shifted, finished, stored = sem("styled"), sem("shifted"), sem("finished"), sem("stored")
        SMALL = 5

        out_v = out.rearrange("b (j p) d -> b p j d", p=P)
        x_v = x_in.rearrange("b (j p) d -> b p j d", p=P)
        c_v = context.rearrange("b (j p) d -> b p j d", p=P)

        with nc.Block() as block:

            @block.sync
            def _(sp):
                def load_xc(b):
                    sp.dma_start(xc[:, 0, :, :], x_v[b]).then_inc(xc_loaded, DMA)
                    sp.dma_start(xc[:, 1, :, :], c_v[b]).then_inc(xc_loaded, DMA)

                def load_keep(b):
                    sp.dma_start(keep_u8[:, :], keep[b]).then_inc(keep_loaded, DMA)

                def stack(b, par, first=False):
                    n_lo = counted_to(sp, 2 * CT * b + 2 * CT)
                    n_rescored = counted_to(sp, 4 * HG * (b - 1))
                    sp.wait_ge(ident_made, 1)
                    sp.wait_ge(qk_lo_made, n_lo)
                    if first:
                        sp.wait_ge(stacks_set, 2 * par + 2)
                    else:
                        sp.wait_ge(rescored, n_rescored)
                    for kind in range(2):
                        dst = (q_stack, k_stack)[kind][par]
                        blocks = ((qk_hi, qk_lo, qk_hi), (qk_hi, qk_hi, qk_lo))[kind]
                        for r, src in enumerate(blocks):
                            for h in range(HT):
                                row = 64 * (h % 2) + D * r
                                sp.dma_start(dst[row:row + D, h // 2::HT // 2, :].bitcast(F32),
                                             src[D * h:D * h + D, 2 * kind:2 * kind + 2, :].bitcast(F32)
                                             ).then_inc(stacked[par], DMA)
                    sp.wait_ge(key_made, b + 1)
                    for e in range(2):
                        row = 64 * e + ROW_MASK
                        sp.dma_start(k_stack[par][row:row + 1, :, :].bitcast(F32),
                                     key_row[:, :].bitcast(F32).unsqueeze(1).to_broadcast([1, NB, T])
                                     ).then_inc(stacked[par], DMA)

                def place_max(b, half, par):
                    sp.wait_ge(max_made, 2 * b + half + 1)
                    for h in range(HT):
                        row = 64 * (h % 2) + ROW_MAX
                        sp.dma_start(q_stack[par][row:row + 2, 4 * half + h // 2, :].bitcast(F32),
                                     max_row[2 * h:2 * h + 2, :].bitcast(F32)
                                     ).then_inc(max_placed[half], DMA)

                def load_final(b):
                    sp.dma_start(xf[:, :, :], x_v[b]).then_inc(xf_loaded, DMA)
                    sp.dma_start(keep_b8[:, :], keep[b].broadcast_to([P, T])).then_inc(keep_b_loaded, DMA)

                def store(b):
                    sp.wait_ge(finished, b + 1)
                    sp.dma_start(out_v[b], xf[:, :, :]).then_inc(stored, DMA)

                for i, w in enumerate((wq, wk, wv)):
                    sp.dma_start(w_nat[:, i, :, :], w.rearrange("(k p) n -> p k n", p=P)
                                 ).then_inc(weights_loaded, DMA)
                load_xc(0)
                load_keep(0)
                for i, w in enumerate((bq, bk)):
                    sp.dma_start(b_col[:, i, :], w).then_inc(consts_loaded, DMA)
                sp.dma_start(bv_row[:, :], bv.broadcast_to([P, C])).then_inc(consts_loaded, DMA)
                load_final(0)
                sp.wait_ge(xc_lo_made, 2)
                load_xc(1)
                stack(0, 0, True)
                sp.wait_ge(stacked[0], STACK_DMAS * DMA)
                load_keep(1)
                place_max(0, 0, 0)
                place_max(0, 1, 0)

                def step(b, par, first=False, second=False, tail=0):
                    if tail < 2:
                        stack(b + 1, 1 - par, first)
                        sp.wait_ge(xc_lo_made, 2 * (b + 2))
                        if tail < 1:
                            load_xc(b + 2)
                            load_keep(b + 2)
                        place_max(b + 1, 0, 1 - par)
                    if not first:
                        store(b - 1)
                        sp.wait_ge(stored, DMA * b)
                        load_final(b)
                    if tail < 2:
                        place_max(b + 1, 1, 1 - par)

                step(0, 0, first=True)
                with sp.Fori(0, (B - 4) // 2) as i:
                    step(2 * i + 1, 1)
                    step(2 * i + 2, 0)
                step(B - 3, 1)
                step(B - 2, 0, tail=1)
                step(B - 1, 1, tail=2)
                store(B - 1)
                sp.wait_ge(stored, DMA * B)

            @block.gpsimd
            def _(pool):
                nc.gpsimd.memset(ident[:, :], 0.0).then_inc(ident_made, 1)
                nc.gpsimd.memset(neg_half[:, :], -0.5).then_inc(ident_made, 1)
                pool.wait_ge(ident_made, 2)
                nc.gpsimd.affine_select(out=ident[:, :], in_=ident[:, :], compare_op=ALU.not_equal,
                                        fill=1.0, base=0, pattern=[[-1, P]], channel_multiplier=1
                                        ).then_inc(ident_made, 1)
                nc.gpsimd.memset(ones[:, :], 1.0).then_inc(ones_made, 1)

                def round_xc(b, first=False):
                    n_xc_loaded = counted_to(pool, 2 * DMA * (b + 1))
                    n_v_summed = counted_to(pool, 2 * b)
                    pool.wait_ge(ident_made, 1)
                    pool.wait_ge(xc_loaded, n_xc_loaded)
                    if not first:
                        pool.wait_ge(v_summed, n_v_summed)
                    for i in range(2):
                        nc.gpsimd.tensor_scalar(xc_hi[:, i, :, :], xc[:, i, :, :], 1.0, 0.0,
                                                ALU.mult, ALU.add).then_inc(xc_hi_made, 1)

                def square_v(b, par):
                    pool.wait_ge(v_made, 2 * b + 2)
                    v = vv[:, par, :, :, 0:D].rearrange("p t h d -> p (t h) d")
                    nc.gpsimd.tensor_tensor(vv[:, par, :, :, D:2 * D].rearrange("p t h d -> p (t h) d"),
                                            v, v, ALU.mult).then_inc(vv_made, 1)

                def move_moments(b, g, first=False):
                    n_moments_made = counted_to(pool, GROUPS * b + g + 1)
                    pool.wait_ge(ident_made, 1)
                    pool.wait_ge(moments_made, n_moments_made)
                    if not first and g == 0:
                        pool.wait_ge(shifted, b)
                        pool.wait_ge(var_made, b)
                    for h in range(4):
                        for i, dst in enumerate((mean, second)):
                            row = D * ((4 * g + h) % HT)
                            src = 2 * D * h + D * i
                            pool.dma_start(dst[row:row + D, g // 2, :], moments[src:src + D, g % 2, :]
                                           ).then_inc(moments_moved[g % 2], DMA)

                def keep_x(b, first=False):
                    n_keep_b_loaded = counted_to(pool, DMA * (b + 1))
                    n_finished = counted_to(pool, b)
                    pool.wait_ge(ident_made, 1)
                    pool.wait_ge(keep_b_loaded, n_keep_b_loaded)
                    if not first:
                        pool.wait_ge(finished, n_finished)
                    nc.gpsimd.tensor_scalar(keep_b[:, :], keep_b8[:, :], 1.0, 0.0, ALU.mult, ALU.add
                                            ).then_inc(keep_b_made, 1)
                    pool.wait_ge(keep_b_made, b + 1)
                    pool.wait_ge(xf_loaded, DMA * (b + 1))
                    nc.gpsimd.tensor_tensor(xf[:, :, :], xf[:, :, :],
                                            keep_b[:, :].unsqueeze(1).to_broadcast([P, CT, T]), ALU.mult
                                            ).then_inc(x_kept, 1)

                def instance_stats(b):
                    pool.wait_ge(counted, b + 1)
                    pool.wait_ge(summed, 4 * (b + 1))
                    rc = small[:, RCNT, 0:1].to_broadcast([P, CT])
                    nc.gpsimd.tensor_tensor(small[:, MEAN, :], sum_x[:, :], rc, ALU.mult).then_inc(small_made, 1)
                    nc.gpsimd.tensor_tensor(small[:, SEC, :], sum_xx[:, :], rc, ALU.mult).then_inc(small_made, 1)
                    pool.wait_ge(small_made, SMALL * b + 2)
                    nc.gpsimd.tensor_tensor(small[:, SQ, :], small[:, MEAN, :], small[:, MEAN, :], ALU.mult
                                            ).then_inc(small_made, 1)
                    pool.wait_ge(small_made, SMALL * b + 3)
                    nc.gpsimd.tensor_tensor(small[:, VAR, :], small[:, SEC, :], small[:, SQ, :], ALU.subtract
                                            ).then_inc(small_made, 1)
                    n_small_made = counted_to(pool, SMALL * b + 4)
                    pool.wait_ge(ident_made, 1)
                    pool.wait_ge(small_made, n_small_made)
                    nc.gpsimd.tensor_scalar(small[:, VAR, :], small[:, VAR, :], 0.0, EPS, ALU.max, ALU.add
                                            ).then_inc(small_made, 1)
                    pool.wait_ge(small_made, SMALL * b + 5)
                    nc.gpsimd.tensor_tensor(small[:, RSTD, :], small[:, VAR, :], neg_half[:, :], ALU.pow
                                            ).then_inc(rstd_made, 1)

                def put_together(b):
                    pool.wait_ge(x_normed, CT * (b + 1))
                    pool.wait_ge(rooted, b + 1)
                    nc.gpsimd.tensor_tensor(xf[:, :, :], xf[:, :, :], work[:, :, :], ALU.mult
                                            ).then_inc(styled, 1)
                    pool.wait_ge(styled, b + 1)
                    nc.gpsimd.tensor_tensor(xf[:, :, :], xf[:, :, :], mean[:, :, :], ALU.add
                                            ).then_inc(shifted, 1)

                def set_ones(par):
                    for part in (q_stack[par], k_stack[par]):
                        nc.gpsimd.memset(part[:, :, :].bitcast(F32), 1.0).then_inc(stacks_set, 1)

                set_ones(0)
                round_xc(0, True)
                set_ones(1)
                square_v(0, 0)
                round_xc(1)
                square_v(1, 1)

                def step(b, par, first=False, second=False, tail=0):
                    if not first:
                        keep_x(b - 1, second)
                        instance_stats(b - 1)
                        put_together(b - 1)
                    move_moments(b, 0, first)
                    if tail < 1:
                        round_xc(b + 2)
                    for g in range(1, GROUPS):
                        move_moments(b, g)
                    if tail < 1:
                        square_v(b + 2, par)

                step(0, 0, first=True)
                step(1, 1, second=True)
                with pool.Fori(1, (B - 2) // 2) as i:
                    step(2 * i, 0)
                    step(2 * i + 1, 1)
                step(B - 2, 0, tail=1)
                step(B - 1, 1, tail=2)
                keep_x(B - 1)
                instance_stats(B - 1)
                put_together(B - 1)

            @block.scalar
            def _(act):
                def round_qk(b, n):
                    act.wait_ge(qk_summed, 2 * CT * b + n + 1)
                    nc.scalar.activation(qk_hi[:, n, :], ps_a[:, n % 2, :], ACT.Identity,
                                         bias=b_col[:, n // 2, n % 2:n % 2 + 1]).then_inc(qk_hi_made, 1)

                def copy_max(b, half_):
                    act.wait_ge(max_turned, 2 * b + half_ + 1)
                    nc.scalar.activation(max_hi[:, :], ps_a[0:2 * HT, 0, :], ACT.Copy).then_inc(max_hi_made, 1)

                def exp_unit(b, w, first=False):
                    hg, h = w // 4, w % 4
                    act.wait_ge(rescored, 4 * HG * b + w + 1)
                    if h == 0 and not (first and hg < 2):
                        act.wait_ge(weighed, HG * b + hg - 1)
                    nc.scalar.activation(probs[:, hg % 2, h, :, :], ps_s[:, w % 2, :, :], ACT.Exp,
                                         scale=SCALE).then_inc(exped, 1)

                def rough_recip(b, g, first=False):
                    act.wait_ge(weighed, HG * b + 2 * g + 2)
                    if not (first and g == 0):
                        act.wait_ge(refined, GROUPS * b + g)
                    nc.scalar.activation(rough[:, :], ps_d[:, :], ACT.Ln).then_inc(log_made, 1)
                    act.wait_ge(log_made, GROUPS * b + g + 1)
                    nc.scalar.activation(rough[:, :], rough[:, :], ACT.Exp, scale=-1.0).then_inc(rough_made, 1)

                def sums(b):
                    act.wait_ge(x_kept, b + 1)
                    for t in range(CT):
                        for f, acc in ((ACT.Copy, sum_x), (ACT.Square, sum_xx)):
                            done = 4 * b + 2 * t + (f == ACT.Square)
                            if not (isinstance(done, int) and done == 0):
                                act.wait_ge(summed, done)
                            nc.scalar.activation(junk[:, :], xf[:, t, :], f, accum_out=acc[:, t:t + 1]
                                                 ).then_inc(summed, 1)

                def square_mean(b):
                    act.wait_ge(moments_moved[0], 2 * OUT_DMAS * DMA * (b + 1))
                    act.wait_ge(moments_moved[1], 2 * OUT_DMAS * DMA * (b + 1))
                    nc.scalar.activation(work[:, :, :], mean[:, :, :], ACT.Square).then_inc(squared, 1)

                def root(b):
                    act.wait_ge(clipped, b + 1)
                    nc.scalar.activation(work[:, :, :], work[:, :, :], ACT.Sqrt).then_inc(rooted, 1)

                act.wait_ge(consts_loaded, DMA * NCONST)
                for n in range(2 * CT):
                    round_qk(0, n)
                copy_max(0, 0)
                copy_max(0, 1)
                act.wait_ge(stacked[0], STACK_DMAS * DMA)
                for n in range(2 * CT):
                    round_qk(1, n)

                def step(b, par, n_before, first=False, tail=0):
                    for s in range(NH):
                        for w in (2 * s, 2 * s + 1):
                            exp_unit(b, w, first)
                        if s == 1 and not first:
                            sums(b - 1)
                        if s == 3 and not first:
                            square_mean(b - 1)
                        if s == 5 and not first:
                            root(b - 1)
                        if s in (6, 10, 14):
                            rough_recip(b, (s - 6) // 4, first)
                        if s == 8 and tail < 2:
                            copy_max(b + 1, 0)
                    if tail < 2:
                        copy_max(b + 1, 1)
                    if tail < 1:
                        act.wait_ge(stacked[1 - par], STACK_DMAS * DMA * n_before)
                        for n in range(2 * CT):
                            round_qk(b + 2, n)
                    rough_recip(b, GROUPS - 1)

                step(0, 0, 1, first=True)
                with act.Fori(0, (B - 4) // 2) as i:
                    step(2 * i + 1, 1, i + 2)
                    step(2 * i + 2, 0, i + 2)
                step(B - 3, 1, (B - 4) // 2 + 2)
                step(B - 2, 0, 0, tail=1)
                step(B - 1, 1, 0, tail=2)
                sums(B - 1)
                square_mean(B - 1)
                root(B - 1)

            @block.vector
            def _(dve):
                def split_xc(b, first=False):
                    for i in range(2):
                        dve.wait_ge(xc_hi_made, 2 * b + i + 1)
                        nc.vector.tensor_tensor(xc_lo[:, i, :, :], xc[:, i, :, :],
                                                xc_hi[:, i, :, :].bitcast(F32), ALU.subtract
                                                ).then_inc(xc_lo_made, 1)

                def key_mask(b):
                    dve.wait_ge(keep_loaded, DMA * (b + 1))
                    nc.vector.tensor_scalar(key_row[:, :], keep_u8[:, :], BIG, -BIG, ALU.mult, ALU.add
                                            ).then_inc(key_made, 1)

                def split_qk(b):
                    for n in range(2 * CT):
                        dve.wait_ge(qk_hi_made, 2 * CT * b + n + 1)
                        nc.vector.scalar_tensor_tensor(
                            out=qk_lo[:, n, :], in0=ps_a[:, n % 2, :],
                            scalar=b_col[:, n // 2, n % 2:n % 2 + 1], in1=qk_hi[:, n, :].bitcast(F32),
                            op0=ALU.add, op1=ALU.subtract).then_inc(qk_lo_made, 1)

                def bias_v_rows(b, par, first=False):
                    if not first:
                        dve.wait_ge(weighed, HG * (b - 1))
                    for i in range(2):
                        dve.wait_ge(v_summed, 2 * b + i + 1)
                        for t in range(2):
                            ins = nc.vector.tensor_tensor(
                                vv[:, par, 2 * i + t, :, 0:D],
                                ps_a[:, i, t * C:t * C + C].rearrange("p (h d) -> p h d", d=D),
                                bv_row[:, :].rearrange("p (h d) -> p h d", d=D), ALU.add)
                        ins.then_inc(v_made, 1)

                def maxima(b, s, first=False):
                    for t in range(TB):
                        dve.wait_ge(scored, TB * (NH * b + s) + t + 1)
                        if s % HT == 0 and t == 0 and not (first and s == 0):
                            dve.wait_ge(mx2_made, (NH // HT) * b + s // HT)
                        nc.vector.tensor_reduce(mx[:, t, s % HT:s % HT + 1], ps_a[:, t % 2, :],
                                                axis=AX.X, op=ALU.max).then_inc(maxed, 1)

                def double_max(b, half, first=False):
                    dve.wait_ge(maxed, TB * (NH * b + HT * (half + 1)))
                    if not (first and half == 0):
                        dve.wait_ge(max_turned, 2 * b + half)
                    nc.vector.tensor_scalar(
                        mx2[:, :, :].rearrange("p t (h e) -> p (t h) e", e=2),
                        mx[:, :, :].rearrange("p t h -> p (t h)").unsqueeze(2)
                        .to_broadcast([P, TB * HT, 2]), -1.0, None, ALU.mult).then_inc(mx2_made, 1)

                def split_max(b, half, first=False):
                    dve.wait_ge(max_hi_made, 2 * b + half + 1)
                    if half == 1:
                        dve.wait_ge(max_placed[0], ROW_DMAS * DMA * (b + 1))
                    elif not first:
                        dve.wait_ge(max_placed[1], ROW_DMAS * DMA * b)
                    nc.vector.scalar_tensor_tensor(
                        out=max_row[:, :], in0=max_hi[:, :].bitcast(F32), scalar=minus_odd[:, 0:1],
                        in1=ps_a[0:2 * HT, 0, :], op0=ALU.mult, op1=ALU.add).then_inc(max_made, 1)

                def refine(b, g, first=False):
                    n = GROUPS * b + g + 1
                    dve.wait_ge(rough_made, n)
                    nc.vector.tensor_tensor(newton[:, :], ps_d[:, :], rough[:, :], ALU.mult
                                            ).then_inc(newton_made, 1)
                    dve.wait_ge(newton_made, n)
                    nc.vector.scalar_tensor_tensor(out=newton[:, :], in0=newton[:, :], scalar=-2.0,
                                                   in1=rough[:, :], op0=ALU.add, op1=ALU.mult
                                                   ).then_inc(refined, 1)
                    dve.wait_ge(refined, n)
                    if not (first and g < 2):
                        k = 2 * b + g // 2
                        dve.wait_ge(moments_moved[g % 2], OUT_DMAS * DMA * k)
                    nc.vector.scalar_tensor_tensor(out=moments[:, g % 2, :], in0=newton[:, :], scalar=-1.0,
                                                   in1=ps_m[:, :], op0=ALU.mult, op1=ALU.mult
                                                   ).then_inc(moments_made, 1)

                def recip_count(b):
                    dve.wait_ge(keep_b_made, b + 1)
                    if not (isinstance(b, int) and b == 0):
                        dve.wait_ge(small_made, SMALL * b)
                    nc.vector.tensor_reduce(count[:, :], keep_b[:, :], axis=AX.X, op=ALU.add
                                            ).then_inc(count_made, 1)
                    dve.wait_ge(count_made, b + 1)
                    nc.vector.reciprocal(small[:, RCNT, 0:1], count[:, :]).then_inc(counted, 1)

                def normalise(b):
                    dve.wait_ge(rstd_made, b + 1)
                    dve.wait_ge(summed, 4 * (b + 1))
                    for t in range(CT):
                        nc.vector.tensor_scalar(xf[:, t, :], xf[:, t, :], small[:, MEAN, t:t + 1],
                                                small[:, RSTD, t:t + 1], ALU.subtract, ALU.mult
                                                ).then_inc(x_normed, 1)

                def variance(b):
                    dve.wait_ge(squared, b + 1)
                    nc.vector.tensor_tensor(work[:, :, :], second[:, :, :], work[:, :, :], ALU.subtract
                                            ).then_inc(var_made, 1)
                    dve.wait_ge(var_made, b + 1)
                    nc.vector.tensor_scalar(work[:, :, :], work[:, :, :], 0.0, None, ALU.max
                                            ).then_inc(clipped, 1)

                def finish(b):
                    dve.wait_ge(shifted, b + 1)
                    nc.vector.tensor_tensor(xf[:, :, :], xf[:, :, :],
                                            keep_b[:, :].unsqueeze(1).to_broadcast([P, CT, T]), ALU.mult
                                            ).then_inc(finished, 1)

                dve.wait_ge(weights_loaded, 3 * DMA)
                for i in range(3):
                    nc.vector.tensor_copy(w_hi[:, i, :, :], w_nat[:, i, :, :]).then_inc(w_hi_made, 1)
                for i in range(3):
                    dve.wait_ge(w_hi_made, i + 1)
                    nc.vector.tensor_tensor(w_lo[:, i, :, :], w_nat[:, i, :, :],
                                            w_hi[:, i, :, :].bitcast(F32), ALU.subtract
                                            ).then_inc(w_lo_made, 1)
                dve.wait_ge(ident_made, 3)
                nc.vector.tensor_reduce(minus_odd[:, :], ident[0:2 * HT, 1:2 * HT:2], axis=AX.X,
                                        op=ALU.add, negate=True).then_inc(odd_made, 1)
                split_xc(0)
                key_mask(0)
                dve.wait_ge(consts_loaded, DMA * NCONST)
                split_qk(0)
                bias_v_rows(0, 0, True)
                split_xc(1)
                dve.wait_ge(odd_made, 1)
                for s in range(NH):
                    maxima(0, s, True)
                    if s % HT == HT - 1:
                        double_max(0, s // HT, True)
                        split_max(0, s // HT, True)
                split_qk(1)
                key_mask(1)
                bias_v_rows(1, 1, True)

                def step(b, par, first=False, tail=0):
                    for s in range(NH):
                        if tail < 2:
                            if s == 8:
                                split_max(b + 1, 0)
                            maxima(b + 1, s)
                            if s % HT == HT - 1:
                                double_max(b + 1, s // HT)
                        if s == 1 and not first:
                            recip_count(b - 1)
                        if s == 3 and not first:
                            normalise(b - 1)
                        if s == 4 and not first:
                            variance(b - 1)
                        if s == 8 and not first:
                            finish(b - 1)
                        if s in (6, 10, 14):
                            refine(b, (s - 6) // 4, first)
                    if tail < 2:
                        split_max(b + 1, 1)
                    if tail < 1:
                        split_xc(b + 2)
                        split_qk(b + 2)
                        key_mask(b + 2)
                    refine(b, GROUPS - 1)
                    if tail < 1:
                        bias_v_rows(b + 2, par)

                step(0, 0, first=True)
                with dve.Fori(0, (B - 4) // 2) as i:
                    step(2 * i + 1, 1)
                    step(2 * i + 2, 0)
                step(B - 3, 1)
                step(B - 2, 0, tail=1)
                step(B - 1, 1, tail=2)
                recip_count(B - 1)
                normalise(B - 1)
                variance(B - 1)
                finish(B - 1)

            @block.tensor
            def _(pe):
                def project_qk(b, first=False):
                    pe.wait_ge(xc_lo_made, 2 * b + 2)
                    for n in range(2 * CT):
                        kind, t = n // 2, n % 2
                        if n == 0 and not first:
                            pe.wait_ge(max_made, 2 * b)
                        if n == 1 and not first:
                            pe.wait_ge(maxed, TB * NH * b)
                        if n >= 2:
                            pe.wait_ge(qk_lo_made, 2 * CT * b + n - 1)
                        m = 0
                        for k in range(CT):
                            for w, a in ((w_hi, xc_hi), (w_lo, xc_hi), (w_hi, xc_lo)):
                                ins = nc.tensor.matmul(ps_a[:, n % 2, :], w[:, kind, k, t * P:t * P + P],
                                                       a[:, kind, k, :], start=(m == 0),
                                                       stop=(m == 3 * CT - 1))
                                m += 1
                        ins.then_inc(qk_summed, 1)

                def project_v(b):
                    for i in range(2):
                        pe.wait_ge(qk_lo_made, 2 * CT * b + 3 + i)
                        for t in range(2):
                            m = 0
                            col = (2 * i + t) * P
                            for k in range(CT):
                                for a, w in ((xc_hi, w_hi), (xc_lo, w_hi), (xc_hi, w_lo)):
                                    ins = nc.tensor.matmul(ps_a[:, i, t * C:t * C + C],
                                                           a[:, 1, k, col:col + P], w[:, 2, k, :],
                                                           start=(m == 0), stop=(m == 3 * CT - 1))
                                    m += 1
                        ins.then_inc(v_summed, 1)

                def scores(b, s, par, fill):
                    base = 64 * (s % 2)
                    if s == 0:
                        pe.wait_ge(stacked[par], STACK_DMAS * DMA * fill)
                    for t in range(TB):
                        if s == 0 and t < 2:
                            pe.wait_ge(v_made, 2 * b + 1 + t)
                        elif s == HT and t == 0:
                            pe.wait_ge(max_made, 2 * b + 1)
                        else:
                            pe.wait_ge(maxed, TB * (NH * b + s) + t - 1)
                        nc.tensor.matmul(ps_a[:, t % 2, :],
                                         q_stack[par][base:base + ROW_MAX, s // 2, t * P:t * P + P],
                                         k_stack[par][base:base + ROW_MAX, s // 2, :],
                                         start=True, stop=True).then_inc(scored, 1)

                def turn_max(b, half):
                    pe.wait_ge(mx2_made, 2 * b + half + 1)
                    for t in range(TB):
                        ins = nc.tensor.transpose(ps_a[0:2 * HT, 0, t * P:t * P + P], mx2[:, t, :],
                                                  ident[:, :])
                    ins.then_inc(max_turned, 1)

                def rescore(b, w, par, first=False):
                    hg, h = w // 4, w % 4
                    head, half = 4 * (hg // 2) + h, hg % 2
                    base = 64 * (head % 2)
                    if w % 16 == 0:
                        pe.wait_ge(max_placed[w // 16], ROW_DMAS * DMA * (b + 1))
                    if not (first and w < 2):
                        pe.wait_ge(exped, 4 * HG * b + w - 1)
                    for i in range(2):
                        col = (2 * half + i) * P
                        ins = nc.tensor.matmul(ps_s[:, w % 2, i, :],
                                               k_stack[par][base:base + ROW_MAX + 2, head // 2, col:col + P],
                                               q_stack[par][base:base + ROW_MAX + 2, head // 2, :],
                                               start=True, stop=True)
                    ins.then_inc(rescored, 1)

                def weigh(b, hg, par, first=False):
                    g, half = hg // 2, hg % 2
                    pe.wait_ge(exped, 4 * (HG * b + hg + 1))
                    if hg == 0:
                        pe.wait_ge(vv_made, b + 1)
                    if half == 0 and not (first and g == 0):
                        pe.wait_ge(moments_made, GROUPS * b + g)
                    for i in range(2):
                        for bank, is_sum in ((ps_m, False), (ps_d, True)):
                            for h in range(4):
                                lhs = ones[:, :] if is_sum else vv[:, par, 2 * half + i, 4 * g + h, :]
                                ins = nc.tensor.matmul(bank[2 * D * h:2 * D * h + 2 * D, :], lhs,
                                                       probs[:, hg % 2, h, i, :],
                                                       start=(half == 0 and i == 0),
                                                       stop=(half == 1 and i == 1))
                    ins.then_inc(weighed, 1)

                pe.wait_ge(w_lo_made, 3)
                pe.wait_ge(ident_made, 3)
                pe.wait_ge(ones_made, 1)
                project_qk(0, True)
                project_v(0)
                for s in range(NH):
                    scores(0, s, 0, 1)
                    if s % HT == HT - 1:
                        turn_max(0, s // HT)
                project_qk(1)
                project_v(1)

                def step(b, par, fill, first=False, tail=0):
                    for s in range(NH):
                        rescore(b, 2 * s, par, first)
                        if s % 2 == 1 and s >= 3:
                            weigh(b, (s - 3) // 2, par, first)
                        rescore(b, 2 * s + 1, par, first)
                        if tail < 2:
                            scores(b + 1, s, 1 - par, fill)
                            if s % HT == HT - 1:
                                turn_max(b + 1, s // HT)
                    if tail < 1:
                        project_qk(b + 2)
                    weigh(b, HG - 1, par, first)
                    if tail < 1:
                        project_v(b + 2)

                step(0, 0, 1, first=True)
                with pe.Fori(0, (B - 4) // 2) as i:
                    step(2 * i + 1, 1, i + 2)
                    step(2 * i + 2, 0, i + 2)
                step(B - 3, 1, (B - 4) // 2 + 2)
                step(B - 2, 0, (B - 4) // 2 + 2, tail=1)
                step(B - 1, 1, 0, tail=2)

        nc.clear_and_free_semaphores(sems)
        nc.all_engine_barrier()


def program(nc, x, context, mask1, mask2, keep, ln1_s, ln1_b, w_qkv1, b_qk1, b_v1, w_o1, b_o1,
            ln2_s, ln2_b, w_qkv2, b_qk2, b_v2, w_o2, b_o2, ln3_s, ln3_b, w1, b1, w2, b2,
            wq, bq, wk, bk, wv, bv, out):
    x1, x2, x3 = (nc.dram_tensor(n, [B, S, H], F32).ap() for n in ("x1", "x2", "x3"))
    attention_phase(nc, "self", False, x, x1, None, mask1, w_qkv1, w_o1, b_qk1, b_v1, b_o1, ln1_s, ln1_b)
    attention_phase(nc, "cross", True, x1, x2, context, mask2, w_qkv2, w_o2, b_qk2, b_v2, b_o2,
                    ln2_s, ln2_b)
    mlp_phase(nc, x2, x3, w1, w2, b1, b2, ln3_s, ln3_b)
    style_phase(nc, x3, context, keep, out, wq, wk, wv, bq, bk, bv)


def laid_out(inputs):
    import numpy as np

    a = {k: np.asarray(v) for k, v in inputs.items()}
    l0 = {k[len("L0_xattn_"):]: v for k, v in a.items() if k.startswith("L0_xattn_")}
    l1 = {k[len("L1_xattn_"):]: v for k, v in a.items() if k.startswith("L1_xattn_")}

    def col(v):
        return v.reshape(-1, P).T

    def row(v):
        return v.reshape(1, -1)

    w_qkv2 = np.concatenate([l0["w_q"], l0["w_kv"]], axis=1)
    b_qkv2 = np.concatenate([l0["b_q"], l0["b_kv"]])
    return {
        "x": a["x"], "context": a["ctx_2048"], "mask1": a["mask_1x1xSxS2_fc1"][0],
        "mask2": a["mask_Bx1xSxS2_ff1"][:, 0], "keep": a["mask_Bx1x2048_bf1"],
        "ln1_s": col(l0["ln1_s"]), "ln1_b": col(l0["ln1_b"]), "w_qkv1": l0["w_qkv"],
        "b_qk1": col(l0["b_qkv"][:2 * H]), "b_v1": row(l0["b_qkv"][2 * H:]),
        "w_o1": l0["w_ao"], "b_o1": row(l0["b_ao"]),
        "ln2_s": col(l0["ln2_s"]), "ln2_b": col(l0["ln2_b"]), "w_qkv2": w_qkv2,
        "b_qk2": col(b_qkv2[:2 * H]), "b_v2": row(b_qkv2[2 * H:]),
        "w_o2": l0["w_co"], "b_o2": row(l0["b_co"]),
        "ln3_s": col(l0["ln3_s"]), "ln3_b": col(l0["ln3_b"]), "w1": l0["w1"], "b1": col(l0["b1"]),
        "w2": l0["w2"], "b2": row(l0["b2"]),
        "wq": l1["Wq"].T, "bq": col(l1["bq"]), "wk": l1["Wk"].T, "bk": col(l1["bk"]),
        "wv": l1["Wv"].T, "bv": row(l1["bv"]),
    }


def kernel(**inputs):
    import numpy as np
    import concourse.bacc as bacc
    from concourse.bass_utils import run_bass_kernel_spmd

    nc = bacc.Bacc("TRN2", target_bir_lowering=False, num_devices=1)
    arrays, args = {}, []
    for name, a in laid_out(inputs).items():
        a = np.ascontiguousarray(a)
        arrays[f"in_{name}"] = a
        args.append(nc.dram_tensor(f"in_{name}", a.shape, mybir.dt.from_np(a.dtype),
                                   kind="ExternalInput").ap())
    args.append(nc.dram_tensor("out_0", (B, S, H), F32, kind="ExternalOutput").ap())
    program(nc, *args)
    r = run_bass_kernel_spmd(nc, [arrays], core_ids=[0])
    return r.results[0]["out_0"]
```

```python
import concourse.bass as bass
from concourse import mybir
from contextlib import ExitStack

F32 = mybir.dt.float32
F32R = mybir.dt.float32r
U8 = mybir.dt.uint8
ALU = mybir.AluOpType
ACT = mybir.ActivationFunctionType
AX = mybir.AxisListType

P = 128
B, S, H = 8, 256, 512
NT = S // P
KT = H // P
NH, HD = 16, 32
HPG = P // HD
F = 4 * H
EPS = 1e-5
DMA = 16


def counted_to(engine, value):
    return value if isinstance(value, int) else engine.to_reg(value)


def attention_phase(nc, name, cross, x_in, x_out, context, mask, w_qkv, w_out, bias_qk, bias_v,
                    bias_o, ln_s, ln_b):
    NQK = 8
    PAIRS = NH // 2
    GROUPS = NH // HPG
    STACK_DMAS = 2 * 3 * HPG
    QK_SLOTS = (3, 4, 6, 7)
    CHUNKS = [(0, (0, 1)), (1, (0, 1)), (0, (2, 3)), (1, (2, 3))]
    with ExitStack() as ctx:
        sems = []

        def sb(n, shape, dtype=F32):
            return ctx.enter_context(nc.sbuf_tensor(f"{name}_{n}", shape, dtype))

        def pb(n, shape):
            return ctx.enter_context(nc.psum_tensor(f"{name}_{n}", shape, F32))

        def sem(n):
            sems.append(nc.alloc_semaphore(f"{name}_{n}"))
            return sems[-1]

        w_hi = sb("w_hi", [P, KT, 3 * H], F32R)
        w_lo = sb("w_lo", [P, KT, 3 * H], F32R)
        wo_hi = sb("wo_hi", [P, KT, H], F32R)
        wo_lo = sb("wo_lo", [P, KT, H], F32R)
        bqk = sb("bqk", [P, NQK])
        bv_row = sb("bv_row", [P, H])
        bo_row = sb("bo_row", [P, H])
        lns = sb("lns", [P, KT])
        lnb = sb("lnb", [P, KT])
        ident = sb("ident", [P, P])
        neg_half = sb("neg_half", [P, NT])
        x_ln = sb("x_ln", [P, NT, H])
        x_res = sb("x_res", [P, NT, H])
        stats = sb("stats", [P, NT, 6])
        mean_var = sb("mean_var", [P, NT, 2])
        rstd = sb("rstd", [P, NT])
        y_hi = sb("y_hi", [P, KT, S], F32R)
        y_lo = sb("y_lo", [P, KT, S], F32R)
        if cross:
            c_nat = sb("c_nat", [P, NT, H])
            c_hi = sb("c_hi", [P, KT, S], F32R)
            c_lo = sb("c_lo", [P, KT, S], F32R)
        qk_hi = sb("qk_hi", [P, NQK, S], F32R)
        qk_lo = sb("qk_lo", [P, NQK, S], F32R)
        q_stack = sb("q_stack", [P, NH, S], F32R)
        k_stack = sb("k_stack", [P, NH, S], F32R)
        v = sb("v", [P, 2, NT, H])
        mask_raw = sb("mask_raw", [P, NT, S])
        mask_mul = sb("mask_mul", [P, NT, S])
        mask_add = sb("mask_add", [P, NT, S])
        NS = 4
        sc = sb("sc", [P, NS, 2, NT, S])
        neg_max = sb("neg_max", [P, NS, 2, NT])
        sums = sb("sums", [P, 2, NT, HPG])
        recip = sb("recip", [P, 2, NT, HPG])
        recip_b = sb("recip_b", [P, NT, HPG, HD])
        probs_t = sb("probs_t", [P, 2, HPG, NT, S])
        recip_t = sb("recip_t", [P, S])
        cx = sb("cx", [P, GROUPS, S])
        cx_hi = sb("cx_hi", [P, GROUPS, S], F32R)
        cx_lo = sb("cx_lo", [P, GROUPS, S], F32R)
        y = x_ln[:, :, :].rearrange("p j d -> p (j d)").rearrange("p (k s) -> p k s", k=KT)
        stage = [probs_t[:, i, :, :, :].rearrange("p h t s -> p (h t s)")
                 .rearrange("p (k n) -> p k n", k=KT) for i in range(2)]

        ps_s = pb("ps_s", [P, 2, NT, S])
        ps_t = pb("ps_t", [P, 2, NT, S])
        ps_r = pb("ps_r", [P, 2 * S])
        ps_c = pb("ps_c", [P, 2 * S])
        ps_p = pb("ps_p", [P, 2, H])
        ps_p4 = ps_p[:, :, :].rearrange("p b (k s) -> p (b k) s", k=2)

        consts_loaded = sem("consts_loaded")
        w_loaded = [sem(f"w_loaded{i}") for i in range(2)]
        w_hi_made, w_lo_made = sem("w_hi_made"), sem("w_lo_made")
        ident_made = sem("ident_made")
        x_loaded, res_loaded, stored = sem("x_loaded"), sem("res_loaded"), sem("stored")
        c_loaded, c_turned = sem("c_loaded"), sem("c_turned")
        c_copied, c_hi_made, c_lo_made = sem("c_copied"), sem("c_hi_made"), sem("c_lo_made")
        mask_loaded, mask_made, mask_mul_made = sem("mask_loaded"), sem("mask_made"), sem("mask_mul_made")
        stats_made, mv_made = sem("stats_made"), sem("mv_made")
        var_made, rstd_made = sem("var_made"), sem("rstd_made")
        z_made, turned, y_made = sem("z_made"), sem("turned"), sem("y_made")
        y_hi_made, y_lo_made = sem("y_hi_made"), sem("y_lo_made")
        qk_summed, qk_hi_made, qk_lo_made = sem("qk_summed"), sem("qk_hi_made"), sem("qk_lo_made")
        stacked = [sem(f"stacked{i}") for i in range(2)]
        v_summed, v_made = sem("v_summed"), sem("v_made")
        scored, multiplied, masked = sem("scored"), sem("multiplied"), sem("masked")
        exped, probs_turned, probs_made = sem("exped"), sem("probs_turned"), sem("probs_made")
        recip_made, recip_spread = sem("recip_made"), sem("recip_spread")
        recip_turned, recip_copied = sem("recip_turned"), sem("recip_copied")
        pv_summed, cx_made = sem("pv_summed"), sem("cx_made")
        cx_hi_made, cx_lo_made = sem("cx_hi_made"), sem("cx_lo_made")
        o_summed, res_biased, x_made = sem("o_summed"), sem("res_biased"), sem("x_made")

        WCHUNKS = 4
        NCONST = 5

        with nc.Block() as block:

            @block.sync
            def _(sp):
                def load_x(b):
                    sp.dma_start(x_ln[:, :, :], x_in[b].rearrange("(j p) d -> p j d", p=P)
                                 ).then_inc(x_loaded, DMA)

                def load_c(b):
                    sp.dma_start(c_nat[:, :, :], context[b].rearrange("(j p) d -> p j d", p=P)
                                 ).then_inc(c_loaded, DMA)

                def load_mask(b):
                    sp.dma_start(mask_raw[:, :, :], mask[b].rearrange("(j p) k -> p j k", p=P)
                                 ).then_inc(mask_loaded, DMA)

                def load_res(b):
                    sp.dma_start(x_res[:, :, :], x_in[b].rearrange("(j p) d -> p j d", p=P)
                                 ).then_inc(res_loaded, DMA)

                def store(b):
                    sp.wait_ge(x_made, NT * b + NT)
                    sp.dma_start(x_out[b].rearrange("(j p) d -> p j d", p=P), x_res[:, :, :]
                                 ).then_inc(stored, DMA)

                def stack(half, b, first=False):
                    n_qk_lo_made = counted_to(sp, NQK * b + 4 * half + 4)
                    n_scored = counted_to(sp, PAIRS * (b - 1) + 4 * half + 4)
                    sp.wait_ge(ident_made, 1)
                    sp.wait_ge(qk_lo_made, n_qk_lo_made)
                    if not first:
                        sp.wait_ge(scored, n_scored)
                    for kind in range(2):
                        n = 2 * (2 * half + kind)
                        dst = (q_stack, k_stack)[kind]
                        blocks = ((qk_hi, qk_lo, qk_hi), (qk_hi, qk_hi, qk_lo))[kind]
                        for r, src in enumerate(blocks):
                            for i in range(HPG):
                                sp.dma_start(
                                    dst[HD * r:HD * r + HD, 8 * half + i:8 * half + 8:HPG, :].bitcast(F32),
                                    src[HD * i:HD * i + HD, n:n + 2, :].bitcast(F32)
                                ).then_inc(stacked[half], DMA)

                def weights(c):
                    if c >= 2:
                        sp.wait_ge(w_lo_made, c - 1)
                    src = w_qkv[:, c * H:c * H + H] if c < 3 else w_out
                    sp.dma_start(stage[c % 2], src.rearrange("(k p) n -> p k n", p=P)
                                 ).then_inc(w_loaded[c % 2], DMA)

                load_x(0)
                weights(0)
                weights(1)
                sp.dma_start(bqk[:, :], bias_qk).then_inc(consts_loaded, DMA)
                sp.dma_start(lns[:, :], ln_s).then_inc(consts_loaded, DMA)
                sp.dma_start(lnb[:, :], ln_b).then_inc(consts_loaded, DMA)
                sp.dma_start(bv_row[:, :], bias_v.broadcast_to([P, H])).then_inc(consts_loaded, DMA)
                sp.dma_start(bo_row[:, :], bias_o.broadcast_to([P, H])).then_inc(consts_loaded, DMA)
                load_mask(0)
                if cross:
                    load_c(0)
                weights(2)
                weights(3)
                sp.wait_ge(c_lo_made if cross else y_lo_made, 1)
                load_x(1)
                stack(0, 0, True)
                stack(1, 0, True)
                load_res(0)
                if cross:
                    sp.wait_ge(c_turned, 2)
                    load_c(1)
                    sp.wait_ge(mask_made, 1)
                    load_mask(1)

                def step(b, first=False, last=False, more=True):
                    if more and not last:
                        if cross:
                            sp.wait_ge(c_turned, 2 * (b + 2))
                            load_c(b + 2)
                        sp.wait_ge(c_lo_made if cross else y_lo_made, b + 2)
                        load_x(b + 2)
                    if not last:
                        stack(0, b + 1)
                    if not first:
                        store(b - 1)
                        sp.wait_ge(stored, DMA * b)
                        load_res(b)
                    if not last:
                        stack(1, b + 1)
                        if cross and more:
                            sp.wait_ge(mask_made, b + 2)
                            load_mask(b + 2)

                step(0, first=True)
                with sp.Fori(1, B - 2) as b:
                    step(b)
                step(B - 2, more=False)
                step(B - 1, last=True)
                store(B - 1)
                sp.wait_ge(stored, DMA * B)

            @block.gpsimd
            def _(pool):
                nc.gpsimd.memset(ident[:, :], 0.0).then_inc(ident_made, 1)
                nc.gpsimd.memset(neg_half[:, :], -0.5).then_inc(ident_made, 1)
                pool.wait_ge(ident_made, 2)
                nc.gpsimd.affine_select(out=ident[:, :], in_=ident[:, :], compare_op=ALU.not_equal,
                                        fill=1.0, base=0, pattern=[[-1, P]], channel_multiplier=1
                                        ).then_inc(ident_made, 1)

                def make_rstd(b):
                    n_mv_made = counted_to(pool, NT * b + NT)
                    n_z_made = counted_to(pool, NT * b)
                    pool.wait_ge(ident_made, 1)
                    pool.wait_ge(mv_made, n_mv_made)
                    if not isinstance(b, int) or b > 0:
                        pool.wait_ge(z_made, n_z_made)
                    nc.gpsimd.tensor_scalar(rstd[:, :], mean_var[:, :, 1], 1.0, EPS, ALU.mult, ALU.add
                                            ).then_inc(var_made, 1)
                    pool.wait_ge(var_made, b + 1)
                    nc.gpsimd.tensor_tensor(rstd[:, :], rstd[:, :], neg_half[:, :], ALU.pow
                                            ).then_inc(rstd_made, 1)

                def round_y(b, first=False):
                    n_y_made = counted_to(pool, KT * b + KT)
                    n_v_summed = counted_to(pool, NT * b)
                    pool.wait_ge(ident_made, 1)
                    pool.wait_ge(y_made, n_y_made)
                    if not first:
                        pool.wait_ge(v_summed, n_v_summed)
                    nc.gpsimd.tensor_scalar(y_hi[:, :, :], y[:, :, :], 1.0, 0.0, ALU.mult, ALU.add
                                            ).then_inc(y_hi_made, 1)

                def round_c(b, first=False):
                    n_c_copied = counted_to(pool, 2 * b + 2)
                    n_v_summed = counted_to(pool, NT * b)
                    pool.wait_ge(ident_made, 1)
                    pool.wait_ge(c_copied, n_c_copied)
                    if not first:
                        pool.wait_ge(v_summed, n_v_summed)
                    nc.gpsimd.tensor_scalar(c_hi[:, :, :], y[:, :, :], 1.0, 0.0, ALU.mult, ALU.add
                                            ).then_inc(c_hi_made, 1)

                def bias_res(b):
                    pool.wait_ge(res_loaded, DMA * b + DMA)
                    nc.gpsimd.tensor_tensor(x_res[:, :, :], x_res[:, :, :],
                                            bo_row[:, :].unsqueeze(1).to_broadcast([P, NT, H]),
                                            ALU.add).then_inc(res_biased, 1)

                def round_cx(b, first=False):
                    n_cx_made = counted_to(pool, GROUPS * b + GROUPS)
                    n_o_summed = counted_to(pool, NT * b)
                    pool.wait_ge(ident_made, 1)
                    pool.wait_ge(cx_made, n_cx_made)
                    if not first:
                        pool.wait_ge(o_summed, n_o_summed)
                    nc.gpsimd.tensor_scalar(cx_hi[:, :, :], cx[:, :, :], 1.0, 0.0, ALU.mult, ALU.add
                                            ).then_inc(cx_hi_made, 1)

                make_rstd(0)
                round_y(0, True)
                if cross:
                    round_c(0, True)
                make_rstd(1)
                pool.wait_ge(consts_loaded, DMA * NCONST)
                bias_res(0)

                def step(b, first=False, last=False, more=True):
                    if not last:
                        round_y(b + 1)
                        if cross:
                            round_c(b + 1)
                    if not first:
                        round_cx(b - 1, isinstance(b, int) and b == 1)
                    if more:
                        make_rstd(b + 2)
                    if not first:
                        bias_res(b)

                step(0, first=True)
                step(1)
                with pool.Fori(2, B - 2) as b:
                    step(b)
                step(B - 2, more=False)
                step(B - 1, last=True, more=False)
                round_cx(B - 1)

            @block.scalar
            def _(act):
                def round_w(c):
                    act.wait_ge(w_loaded[c % 2], DMA * (c // 2 + 1))
                    dst = w_hi[:, :, c * H:c * H + H] if c < 3 else wo_hi[:, :, :]
                    nc.scalar.activation(dst, stage[c % 2], ACT.Copy).then_inc(w_hi_made, 1)

                def scale_y(b):
                    for k in range(KT):
                        if k == 0:
                            act.wait_ge(turned, 2 * b + 2)
                        nc.scalar.activation(y[:, k, :], ps_p4[:, k, :], ACT.Identity,
                                             bias=lnb[:, k:k + 1], scale=lns[:, k:k + 1]
                                             ).then_inc(y_made, 1)

                def copy_c(b):
                    act.wait_ge(y_lo_made, b + 1)
                    for i in range(2):
                        act.wait_ge(c_turned, 2 * b + i + 1)
                        nc.scalar.activation(y[:, 2 * i:2 * i + 2, :], ps_p4[:, 2 * i:2 * i + 2, :],
                                             ACT.Copy).then_inc(c_copied, 1)

                def round_qk(b, c, first=False):
                    kind, tiles = CHUNKS[c]
                    for i, t in enumerate(tiles):
                        n = 2 * c + i
                        act.wait_ge(qk_summed, NQK * b + n + 1)
                        if i == 0 and c % 2 == 0 and not first:
                            act.wait_ge(stacked[c // 2], STACK_DMAS * DMA * b)
                        col = 4 * kind + t
                        nc.scalar.activation(qk_hi[:, n, :], ps_p[:, i, 0:S], ACT.Identity,
                                             bias=bqk[:, col:col + 1]).then_inc(qk_hi_made, 1)

                def exps(b, u, first=False):
                    if u % 2 == 0 and not (first and u < 4):
                        act.wait_ge(recip_made, GROUPS * b + u // 2 - 1)
                    for i in range(4):
                        h, t = i // 2, i % 2
                        act.wait_ge(masked, 4 * (PAIRS * b + u) + i + 1)
                        col = 2 * (u % 2) + h
                        nc.scalar.activation(sc[:, u % NS, h, t, :], sc[:, u % NS, h, t, :], ACT.Exp,
                                             bias=neg_max[:, u % NS, h, t:t + 1], scale=-1.0,
                                             accum_out=sums[:, (u // 2) % 2, t, col:col + 1]
                                             ).then_inc(exped, 1)

                def copy_probs(b, u, first=False):
                    g = u // 2
                    if u % 2 == 0 and not (first and g < 2):
                        act.wait_ge(pv_summed, GROUPS * b + g - 1)
                    act.wait_ge(probs_turned, 2 * (PAIRS * b + u) + 2)
                    nc.scalar.activation(probs_t[:, g % 2, 2 * (u % 2):2 * (u % 2) + 2, :, :],
                                         ps_t[:, :, :, :], ACT.Copy).then_inc(probs_made, 1)

                def copy_recip(b, g):
                    act.wait_ge(recip_turned, GROUPS * b + g + 1)
                    if not (isinstance(b, int) and b == 0 and g == 0):
                        act.wait_ge(cx_made, GROUPS * b + g)
                    nc.scalar.activation(recip_t[:, :], ps_r[:, 0:S], ACT.Copy).then_inc(recip_copied, 1)

                for c in range(WCHUNKS):
                    round_w(c)
                act.wait_ge(consts_loaded, DMA * NCONST)
                scale_y(0)
                if cross:
                    copy_c(0)
                for c in range(4):
                    round_qk(0, c, True)
                act.wait_ge(w_lo_made, WCHUNKS)

                def step(b, first=False, last=False):
                    for u in range(PAIRS):
                        if u == 7 and not last:
                            round_qk(b + 1, 3)
                        if u >= 2:
                            copy_probs(b, u - 2, first)
                        elif not first:
                            copy_probs(b - 1, PAIRS - 2 + u)
                        exps(b, u, first)
                        if u in (0, 2) and not first:
                            copy_recip(b - 1, GROUPS - 2 + u // 2)
                        if u in (4, 6):
                            copy_recip(b, (u - 4) // 2)
                        if u == 1 and not last:
                            scale_y(b + 1)
                        if u == 2 and cross and not last:
                            copy_c(b + 1)
                        if u in QK_SLOTS[:3] and not last:
                            round_qk(b + 1, QK_SLOTS.index(u))

                step(0, first=True)
                with act.Fori(1, B - 1) as b:
                    step(b)
                step(B - 1, last=True)
                for i in range(2):
                    copy_probs(B - 1, PAIRS - 2 + i)
                    copy_recip(B - 1, GROUPS - 2 + i)

            @block.vector
            def _(dve):
                def split_w(c):
                    dve.wait_ge(w_hi_made, c + 1)
                    hi = w_hi[:, :, c * H:c * H + H] if c < 3 else wo_hi[:, :, :]
                    lo = w_lo[:, :, c * H:c * H + H] if c < 3 else wo_lo[:, :, :]
                    nc.vector.tensor_tensor(lo, stage[c % 2], hi.bitcast(F32), ALU.subtract
                                            ).then_inc(w_lo_made, 1)

                def norm_stats(b):
                    dve.wait_ge(x_loaded, DMA * b + DMA)
                    for j in range(NT):
                        nc.vector.bn_stats(stats[:, j, :], x_ln[:, j, :]).then_inc(stats_made, 1)
                    for j in range(NT):
                        n_stats_made = counted_to(dve, NT * b + j + 1)
                        dve.wait_ge(ident_made, 1)
                        dve.wait_ge(stats_made, n_stats_made)
                        nc.vector.bn_aggr(mean_var[:, j, :], stats[:, j, :]).then_inc(mv_made, 1)

                def normalise(b):
                    dve.wait_ge(rstd_made, b + 1)
                    for j in range(NT):
                        nc.vector.tensor_scalar(x_ln[:, j, :], x_ln[:, j, :], mean_var[:, j, 0:1],
                                                rstd[:, j:j + 1], ALU.subtract, ALU.mult
                                                ).then_inc(z_made, 1)

                def split_y(b):
                    dve.wait_ge(y_hi_made, b + 1)
                    nc.vector.tensor_tensor(y_lo[:, :, :], y[:, :, :], y_hi[:, :, :].bitcast(F32),
                                            ALU.subtract).then_inc(y_lo_made, 1)

                def split_c(b):
                    dve.wait_ge(c_hi_made, b + 1)
                    nc.vector.tensor_tensor(c_lo[:, :, :], y[:, :, :], c_hi[:, :, :].bitcast(F32),
                                            ALU.subtract).then_inc(c_lo_made, 1)

                def split_qk(b, c):
                    kind, tiles = CHUNKS[c]
                    for i, t in enumerate(tiles):
                        n = 2 * c + i
                        dve.wait_ge(qk_hi_made, NQK * b + n + 1)
                        col = 4 * kind + t
                        nc.vector.scalar_tensor_tensor(
                            out=qk_lo[:, n, :], in0=ps_p[:, i, 0:S], scalar=bqk[:, col:col + 1],
                            in1=qk_hi[:, n, :].bitcast(F32), op0=ALU.add, op1=ALU.subtract
                        ).then_inc(qk_lo_made, 1)

                def bias_v_rows(b, par, first=False):
                    if not first:
                        dve.wait_ge(pv_summed, GROUPS * (b - 1))
                    for j in range(NT):
                        dve.wait_ge(v_summed, NT * b + j + 1)
                        nc.vector.tensor_tensor(v[:, par, j, :], ps_p[:, j, :], bv_row[:, :], ALU.add
                                                ).then_inc(v_made, 1)

                def make_mask(b):
                    dve.wait_ge(mask_loaded, DMA * b + DMA)
                    if not (isinstance(b, int) and b == 0):
                        dve.wait_ge(masked, 4 * PAIRS * b)
                    nc.vector.tensor_scalar(mask_mul[:, :, :], mask_raw[:, :, :], HD ** -0.5, None,
                                            ALU.mult).then_inc(mask_mul_made, 1)
                    nc.vector.tensor_scalar(mask_add[:, :, :], mask_raw[:, :, :], 10000.0, -10000.0,
                                            ALU.mult, ALU.add).then_inc(mask_made, 1)

                def mask_scores(b, u, first=False):
                    if u == 0 and (first or cross):
                        dve.wait_ge(mask_made, b + 1)
                    dve.wait_ge(scored, PAIRS * b + u + 1)
                    if not (first and u < NS):
                        dve.wait_ge(probs_turned, 2 * (PAIRS * b + u - NS + 1))
                    s = u % NS
                    nc.vector.tensor_tensor(
                        sc[:, s, :, :, :].rearrange("p h t k -> p h (t k)"),
                        ps_s[:, :, :, :].rearrange("p h t k -> p h (t k)"),
                        mask_mul[:, :, :].rearrange("p t k -> p (t k)").unsqueeze(1)
                        .to_broadcast([P, 2, NT * S]), ALU.mult).then_inc(multiplied, 1)
                    n_multiplied = counted_to(dve, PAIRS * b + u + 1)
                    dve.wait_ge(ident_made, 1)
                    dve.wait_ge(multiplied, n_multiplied)
                    for i in range(4):
                        h, t = i // 2, i % 2
                        nc.vector.tensor_tensor_reduce(
                            out=sc[:, s, h, t, :], in0=sc[:, s, h, t, :], in1=mask_add[:, t, :],
                            scale=-1.0, scalar=3e38, op0=ALU.add, op1=ALU.min,
                            accum_out=neg_max[:, s, h, t:t + 1]).then_inc(masked, 1)

                def recips(b, g):
                    dve.wait_ge(exped, 4 * (PAIRS * b + 2 * g + 2))
                    nc.vector.reciprocal(recip[:, g % 2, :, :], sums[:, g % 2, :, :]).then_inc(recip_made, 1)
                    dve.wait_ge(recip_made, GROUPS * b + g + 1)
                    if not (isinstance(b, int) and b == 0 and g == 0):
                        dve.wait_ge(recip_turned, GROUPS * b + g)
                    nc.vector.tensor_copy(recip_b[:, :, :, :].rearrange("p t h d -> p (t h) d"),
                                          recip[:, g % 2, :, :].rearrange("p t h -> p (t h)")
                                          .unsqueeze(2).to_broadcast([P, NT * HPG, HD])
                                          ).then_inc(recip_spread, 1)

                def scale_cx(b, g, first=False):
                    if g == 0 and not first:
                        dve.wait_ge(cx_lo_made, b)
                    dve.wait_ge(pv_summed, GROUPS * b + g + 1)
                    dve.wait_ge(recip_copied, GROUPS * b + g + 1)
                    nc.vector.tensor_tensor(cx[:, g, :], ps_c[:, 0:S], recip_t[:, :], ALU.mult
                                            ).then_inc(cx_made, 1)

                def split_cx(b):
                    dve.wait_ge(cx_hi_made, b + 1)
                    nc.vector.tensor_tensor(cx_lo[:, :, :], cx[:, :, :], cx_hi[:, :, :].bitcast(F32),
                                            ALU.subtract).then_inc(cx_lo_made, 1)

                def add_res(b):
                    dve.wait_ge(res_biased, b + 1)
                    for j in range(NT):
                        dve.wait_ge(o_summed, NT * b + j + 1)
                        nc.vector.tensor_tensor(x_res[:, j, :], ps_p[:, j, :], x_res[:, j, :], ALU.add
                                                ).then_inc(x_made, 1)

                norm_stats(0)
                normalise(0)
                for c in range(WCHUNKS):
                    split_w(c)
                split_y(0)
                if cross:
                    split_c(0)
                for c in range(4):
                    split_qk(0, c)
                dve.wait_ge(consts_loaded, DMA * NCONST)
                bias_v_rows(0, 0, True)
                make_mask(0)
                norm_stats(1)
                normalise(1)

                def step(b, par, first=False, last=False, more=True, second=False):
                    for u in range(PAIRS):
                        mask_scores(b, u, first)
                        if u == 0 and not first:
                            bias_v_rows(b, par, second)
                        if u == 1 and not first:
                            recips(b - 1, GROUPS - 1)
                        if u in (3, 5, 7):
                            recips(b, (u - 3) // 2)
                        if u in (1, 3) and not first:
                            scale_cx(b - 1, GROUPS - 2 + u // 2, False)
                        if u in (5, 7):
                            scale_cx(b, (u - 5) // 2, first)
                        if u == 2 and not last:
                            split_y(b + 1)
                        if u == 3 and cross and not last:
                            split_c(b + 1)
                        if u == 4 and not first:
                            split_cx(b - 1)
                        if u in QK_SLOTS and not last:
                            split_qk(b + 1, QK_SLOTS.index(u))
                        if more and u == 5:
                            norm_stats(b + 2)
                        if u == 5 and not first:
                            add_res(b - 1)
                        if more and u == 6:
                            normalise(b + 2)
                    if cross and not last:
                        make_mask(b + 1)

                step(0, 0, first=True)
                step(1, 1, second=True)
                with dve.Fori(1, (B - 2) // 2) as i:
                    step(2 * i, 0)
                    step(2 * i + 1, 1)
                step(B - 2, 0, more=False)
                step(B - 1, 1, last=True, more=False)
                scale_cx(B - 1, GROUPS - 2)
                recips(B - 1, GROUPS - 1)
                scale_cx(B - 1, GROUPS - 1)
                split_cx(B - 1)
                add_res(B - 1)

            @block.tensor
            def _(pe):
                def passes(out, lhs, rhs, l_slice, r_slice, steps, done):
                    n = 0
                    for k in range(steps):
                        for a, w in ((0, 0), (1, 0), (0, 1)):
                            ins = nc.tensor.matmul(out, l_slice(lhs[a], k), r_slice(rhs[w], k),
                                                   start=(n == 0), stop=(n == 3 * steps - 1))
                            n += 1
                    ins.then_inc(done, 1)

                def turn(src, done):
                    for i in range(2):
                        for k in (2 * i, 2 * i + 1):
                            for j in range(NT):
                                ins = nc.tensor.transpose(ps_p4[:, k, j * P:j * P + P],
                                                          src[:, j, k * P:k * P + P], ident[:, :])
                        ins.then_inc(done, 1)

                def turn_x(b, first=False):
                    if first:
                        pe.wait_ge(ident_made, 3)
                    else:
                        pe.wait_ge(v_made, NT * b)
                    pe.wait_ge(z_made, NT * b + NT)
                    turn(x_ln, turned)

                def turn_c(b):
                    pe.wait_ge(c_loaded, DMA * b + DMA)
                    pe.wait_ge(y_made, KT * b + KT)
                    turn(c_nat, c_turned)

                def project_qk(b, c, after_o=None):
                    kind, tiles = CHUNKS[c]
                    src = (c_hi, c_lo) if cross and kind else (y_hi, y_lo)
                    if c == 0:
                        pe.wait_ge(y_lo_made, b + 1)
                        if cross:
                            pe.wait_ge(c_copied, 2 * b + 2)
                    if c == 2 and after_o is not None:
                        pe.wait_ge(x_made, NT * after_o + NT)
                    if c == 1 and cross:
                        pe.wait_ge(c_lo_made, b + 1)
                    for i, t in enumerate(tiles):
                        if c > 0:
                            pe.wait_ge(qk_lo_made, NQK * b + 2 * c - 1 + i)
                        col = (4 * kind + t) * P
                        passes(ps_p[:, i, 0:S], (w_hi, w_lo), src, lambda w, k: w[:, k, col:col + P],
                               lambda a, k: a[:, k, :], KT, qk_summed)

                def project_v(b):
                    src = (c_hi, c_lo) if cross else (y_hi, y_lo)
                    for j in range(NT):
                        pe.wait_ge(qk_lo_made, NQK * b + NQK - 1 + j)
                        passes(ps_p[:, j, :], src, (w_hi, w_lo), lambda a, k: a[:, k, j * P:j * P + P],
                               lambda w, k: w[:, k, 2 * H:3 * H], KT, v_summed)

                def project_o(b):
                    pe.wait_ge(cx_lo_made, b + 1)
                    for j in range(NT):
                        passes(ps_p[:, j, :], (cx_hi, cx_lo), (wo_hi, wo_lo),
                               lambda a, k: a[:, k, j * P:j * P + P], lambda w, k: w[:, k, :],
                               KT, o_summed)

                def scores(b, u, first=False):
                    if u % 4 == 0:
                        pe.wait_ge(stacked[u // 4], STACK_DMAS * DMA * (b + 1))
                    if not (first and u == 0):
                        pe.wait_ge(multiplied, PAIRS * b + u)
                    for h in range(2):
                        for t in range(NT):
                            ins = nc.tensor.matmul(ps_s[:, h, t, :],
                                                   q_stack[0:3 * HD, 2 * u + h, t * P:t * P + P],
                                                   k_stack[0:3 * HD, 2 * u + h, :], start=True, stop=True)
                    ins.then_inc(scored, 1)

                def turn_probs(b, u, first=False):
                    pe.wait_ge(exped, 4 * (PAIRS * b + u) + 4)
                    if not (first and u == 0):
                        pe.wait_ge(probs_made, PAIRS * b + u)
                    for h in range(2):
                        for k in range(NT):
                            for t in range(NT):
                                ins = nc.tensor.transpose(ps_t[:, h, k, t * P:t * P + P],
                                                          sc[:, u % NS, h, t, k * P:k * P + P],
                                                          ident[:, :])
                        ins.then_inc(probs_turned, 1)

                def weigh_v(b, g, par, first=False):
                    pe.wait_ge(recip_spread, GROUPS * b + g + 1)
                    if not (first and g == 0):
                        pe.wait_ge(recip_copied, GROUPS * b + g)
                    for t in range(NT):
                        ins = nc.tensor.transpose(ps_r[:, t * P:t * P + P],
                                                  recip_b[:, t, :, :].rearrange("p h d -> p (h d)"),
                                                  ident[:, :])
                    ins.then_inc(recip_turned, 1)
                    pe.wait_ge(probs_made, PAIRS * b + 2 * g + 2)
                    if g == 0:
                        pe.wait_ge(v_made, NT * b + NT)
                    if not (first and g == 0):
                        pe.wait_ge(cx_made, GROUPS * b + g)
                    for k in range(NT):
                        for h in range(HPG):
                            ins = nc.tensor.matmul(
                                ps_c[HD * h:HD * h + HD, 0:S],
                                v[:, par, k, (HPG * g + h) * HD:(HPG * g + h) * HD + HD],
                                probs_t[:, g % 2, h, k, :], start=(k == 0), stop=(k == NT - 1))
                    ins.then_inc(pv_summed, 1)

                turn_x(0, True)
                if cross:
                    turn_c(0)
                pe.wait_ge(w_lo_made, WCHUNKS)
                for c in range(4):
                    project_qk(0, c)
                project_v(0)

                def step(b, par, first=False, last=False):
                    for u in range(PAIRS):
                        scores(b, u, first)
                        if u == 7 and not last:
                            project_qk(b + 1, 3)
                        if u >= 2:
                            turn_probs(b, u - 2, first)
                        elif not first:
                            turn_probs(b - 1, PAIRS - 2 + u)
                        if u == 1 and not last:
                            turn_x(b + 1)
                        if u in (0, 2) and not first:
                            weigh_v(b - 1, GROUPS - 2 + u // 2, 1 - par)
                        if u in (4, 6):
                            weigh_v(b, (u - 4) // 2, par, first)
                        if u == 2 and cross and not last:
                            turn_c(b + 1)
                        if u == 5 and not first:
                            if last:
                                pe.wait_ge(v_made, NT * b + NT)
                            else:
                                pe.wait_ge(qk_lo_made, NQK * b + NQK + 4)
                            project_o(b - 1)
                        if u in QK_SLOTS[:3] and not last:
                            project_qk(b + 1, QK_SLOTS.index(u), None if first else b - 1)
                    if not last:
                        project_v(b + 1)

                step(0, 0, first=True)
                with pe.Fori(0, (B - 2) // 2) as i:
                    step(2 * i + 1, 1)
                    step(2 * i + 2, 0)
                step(B - 1, 1, last=True)
                for i in range(2):
                    turn_probs(B - 1, PAIRS - 2 + i)
                    weigh_v(B - 1, GROUPS - 2 + i, 1)
                pe.wait_ge(x_made, NT * (B - 1))
                project_o(B - 1)

        nc.clear_and_free_semaphores(sems)
        nc.all_engine_barrier()


def mlp_phase(nc, x_in, x_out, w1, w2, b1, b2, ln_s, ln_b):
    name = "mlp"
    MT = F // P
    M = MT // 2
    LAG = 2
    RING = 4
    NCONST = 4
    with ExitStack() as ctx:
        sems = []

        def sb(n, shape, dtype=F32):
            return ctx.enter_context(nc.sbuf_tensor(f"{name}_{n}", shape, dtype))

        def pb(n, shape):
            return ctx.enter_context(nc.psum_tensor(f"{name}_{n}", shape, F32))

        def sem(n):
            sems.append(nc.alloc_semaphore(f"{name}_{n}"))
            return sems[-1]

        w1_hi = sb("w1_hi", [P, KT, F], F32R)
        w1_lo = sb("w1_lo", [P, KT, F], F32R)
        w2_hi = sb("w2_hi", [P, MT, H], F32R)
        w2_lo = sb("w2_lo", [P, MT, H], F32R)
        stage = sb("stage", [P, 2, KT, H])
        b1_col = sb("b1_col", [P, MT])
        b2_row = sb("b2_row", [P, H])
        lns = sb("lns", [P, KT])
        lnb = sb("lnb", [P, KT])
        ident = sb("ident", [P, P])
        neg_half = sb("neg_half", [P, NT])
        x_ln = sb("x_ln", [P, NT, H])
        x_res = sb("x_res", [P, NT, H])
        stats = sb("stats", [P, NT, 6])
        mean_var = sb("mean_var", [P, NT, 2])
        rstd = sb("rstd", [P, NT])
        y = sb("y", [P, KT, S])
        y_hi = sb("y_hi", [P, 2, KT, S], F32R)
        y_lo = sb("y_lo", [P, 2, KT, S], F32R)
        g = sb("g", [P, 2, 2, S])
        g_hi = sb("g_hi", [P, RING, 2, S], F32R)
        g_lo = sb("g_lo", [P, RING, 2, S], F32R)

        ps_h = pb("ps_h", [P, 2, 2, S])
        ps_o = pb("ps_o", [P, 2, NT, H])
        ps_x = pb("ps_x", [P, KT, S])

        consts_loaded, ident_made = sem("consts_loaded"), sem("ident_made")
        w_loaded = [sem(f"w_loaded{i}") for i in range(2)]
        w_hi_made, w_lo_made = sem("w_hi_made"), sem("w_lo_made")
        x_loaded, res_loaded, stored = sem("x_loaded"), sem("res_loaded"), sem("stored")
        stats_made, mv_made = sem("stats_made"), sem("mv_made")
        var_made, rstd_made = sem("var_made"), sem("rstd_made")
        z_made, turned, y_made = sem("z_made"), sem("turned"), sem("y_made")
        y_hi_made, y_lo_made = sem("y_hi_made"), sem("y_lo_made")
        h_summed, g_made = sem("h_summed"), sem("g_made")
        g_hi_made, g_lo_made = sem("g_hi_made"), sem("g_lo_made")
        o_added, res_biased, x_made = sem("o_added"), sem("res_biased"), sem("x_made")

        WCHUNKS = 8

        def w_dst(w1_part, w2_part, c):
            return w1_part[:, :, c * H:c * H + H] if c < 4 else w2_part[:, 4 * (c - 4):4 * (c - 4) + 4, :]

        with nc.Block() as block:

            @block.sync
            def _(sp):
                def load_x(b):
                    sp.dma_start(x_ln[:, :, :], x_in[b].rearrange("(j p) d -> p j d", p=P)
                                 ).then_inc(x_loaded, DMA)

                def load_res(b):
                    sp.dma_start(x_res[:, :, :], x_in[b].rearrange("(j p) d -> p j d", p=P)
                                 ).then_inc(res_loaded, DMA)

                def store(b):
                    sp.wait_ge(x_made, NT * b + NT)
                    sp.dma_start(x_out[b].rearrange("(j p) d -> p j d", p=P), x_res[:, :, :]
                                 ).then_inc(stored, DMA)

                load_x(0)
                for c in range(WCHUNKS):
                    if c >= 2:
                        sp.wait_ge(w_lo_made, c - 1)
                    src = w1[:, c * H:c * H + H] if c < 4 else w2[(c - 4) * H:(c - 3) * H, :]
                    sp.dma_start(stage[:, c % 2, :, :], src.rearrange("(k p) n -> p k n", p=P)
                                 ).then_inc(w_loaded[c % 2], DMA)
                    if c == 1:
                        sp.dma_start(lns[:, :], ln_s).then_inc(consts_loaded, DMA)
                        sp.dma_start(lnb[:, :], ln_b).then_inc(consts_loaded, DMA)
                        sp.dma_start(b1_col[:, :], b1).then_inc(consts_loaded, DMA)
                        sp.dma_start(b2_row[:, :], b2.broadcast_to([P, H])).then_inc(consts_loaded, DMA)
                load_res(0)
                sp.wait_ge(turned, 2)
                load_x(1)

                def step(b, first=False, last=False):
                    if not first:
                        store(b - 1)
                        sp.wait_ge(stored, DMA * b)
                        load_res(b)
                    if not last:
                        sp.wait_ge(turned, 2 * (b + 2))
                        load_x(b + 2)

                step(0, first=True)
                with sp.Fori(1, B - 2) as b:
                    step(b)
                step(B - 2, last=True)
                step(B - 1, last=True)
                store(B - 1)
                sp.wait_ge(stored, DMA * B)

            @block.gpsimd
            def _(pool):
                nc.gpsimd.memset(ident[:, :], 0.0).then_inc(ident_made, 1)
                nc.gpsimd.memset(neg_half[:, :], -0.5).then_inc(ident_made, 1)
                pool.wait_ge(ident_made, 2)
                nc.gpsimd.affine_select(out=ident[:, :], in_=ident[:, :], compare_op=ALU.not_equal,
                                        fill=1.0, base=0, pattern=[[-1, P]], channel_multiplier=1
                                        ).then_inc(ident_made, 1)

                def make_rstd(b, first=False):
                    n_mv_made = counted_to(pool, NT * b + NT)
                    n_z_made = counted_to(pool, NT * b)
                    pool.wait_ge(ident_made, 1)
                    pool.wait_ge(mv_made, n_mv_made)
                    if not first:
                        pool.wait_ge(z_made, n_z_made)
                    nc.gpsimd.tensor_scalar(rstd[:, :], mean_var[:, :, 1], 1.0, EPS, ALU.mult, ALU.add
                                            ).then_inc(var_made, 1)
                    pool.wait_ge(var_made, b + 1)
                    nc.gpsimd.tensor_tensor(rstd[:, :], rstd[:, :], neg_half[:, :], ALU.pow
                                            ).then_inc(rstd_made, 1)

                def round_y(b, par, early=False):
                    n_y_made = counted_to(pool, KT * b + KT)
                    n_h_summed = counted_to(pool, M * (b - 1))
                    pool.wait_ge(ident_made, 1)
                    pool.wait_ge(y_made, n_y_made)
                    if not early:
                        pool.wait_ge(h_summed, n_h_summed)
                    nc.gpsimd.tensor_scalar(y_hi[:, par, :, :], y[:, :, :], 1.0, 0.0, ALU.mult, ALU.add
                                            ).then_inc(y_hi_made, 1)

                def round_g(b, m, first=False):
                    n_g_made = counted_to(pool, 2 * (M * b + m) + 2)
                    n_o_added = counted_to(pool, M * b + m - RING + 1)
                    pool.wait_ge(ident_made, 1)
                    pool.wait_ge(g_made, n_g_made)
                    if not (first and m < RING):
                        pool.wait_ge(o_added, n_o_added)
                    nc.gpsimd.tensor_scalar(g_hi[:, m % RING, :, :], g[:, m % 2, :, :], 1.0, 0.0,
                                            ALU.mult, ALU.add).then_inc(g_hi_made, 1)

                make_rstd(0, True)
                round_y(0, 0, True)

                def step(b, par, first=False, last=False):
                    for m in range(M):
                        round_g(b, m, first)
                        if m == 2:
                            pool.wait_ge(res_loaded, DMA * b + DMA)
                            if first:
                                pool.wait_ge(consts_loaded, DMA * NCONST)
                            nc.gpsimd.tensor_tensor(x_res[:, :, :], x_res[:, :, :],
                                                    b2_row[:, :].unsqueeze(1).to_broadcast([P, NT, H]),
                                                    ALU.add).then_inc(res_biased, 1)
                        if m == 3 and not last:
                            make_rstd(b + 1)
                        if m == 6 and not last:
                            round_y(b + 1, 1 - par, first)

                step(0, 0, first=True)
                with pool.Fori(0, (B - 2) // 2) as i:
                    step(2 * i + 1, 1)
                    step(2 * i + 2, 0)
                step(B - 1, 1, last=True)

            @block.scalar
            def _(act):
                def round_w(c):
                    act.wait_ge(w_loaded[c % 2], DMA * (c // 2 + 1))
                    nc.scalar.activation(w_dst(w1_hi, w2_hi, c), stage[:, c % 2, :, :], ACT.Copy
                                         ).then_inc(w_hi_made, 1)

                def scale_y(b, first=False):
                    for k in range(KT):
                        if k % 2 == 0:
                            act.wait_ge(turned, 2 * b + k // 2 + 1)
                        if k == 0 and not first:
                            act.wait_ge(y_lo_made, b)
                        nc.scalar.activation(y[:, k, :], ps_x[:, k, :], ACT.Identity,
                                             bias=lnb[:, k:k + 1], scale=lns[:, k:k + 1]
                                             ).then_inc(y_made, 1)

                def gelus(b, m, first=False):
                    act.wait_ge(h_summed, M * b + m + 1)
                    if not (first and m < 2):
                        act.wait_ge(g_lo_made, M * b + m - 1)
                    for i in range(2):
                        nc.scalar.activation(g[:, m % 2, i, :], ps_h[:, m % 2, i, :],
                                             ACT.Gelu_apprx_tanh, bias=b1_col[:, 2 * m + i:2 * m + i + 1]
                                             ).then_inc(g_made, 1)

                act.wait_ge(consts_loaded, DMA * NCONST)
                scale_y(0, True)
                for c in range(4):
                    round_w(c)

                def step(b, first=False, last=False):
                    for m in range(M):
                        gelus(b, m, first)
                        if first and m < 4:
                            round_w(4 + m)
                        if m == 5 and not last:
                            scale_y(b + 1)

                step(0, first=True)
                with act.Fori(1, B - 1) as b:
                    step(b)
                step(B - 1, last=True)

            @block.vector
            def _(dve):
                def split_w(c):
                    dve.wait_ge(w_hi_made, c + 1)
                    nc.vector.tensor_tensor(w_dst(w1_lo, w2_lo, c), stage[:, c % 2, :, :],
                                            w_dst(w1_hi, w2_hi, c).bitcast(F32), ALU.subtract
                                            ).then_inc(w_lo_made, 1)

                def norm_stats(b):
                    dve.wait_ge(x_loaded, DMA * b + DMA)
                    for j in range(NT):
                        nc.vector.bn_stats(stats[:, j, :], x_ln[:, j, :]).then_inc(stats_made, 1)
                    for j in range(NT):
                        n_stats_made = counted_to(dve, NT * b + j + 1)
                        dve.wait_ge(ident_made, 1)
                        dve.wait_ge(stats_made, n_stats_made)
                        nc.vector.bn_aggr(mean_var[:, j, :], stats[:, j, :]).then_inc(mv_made, 1)

                def normalise(b):
                    dve.wait_ge(rstd_made, b + 1)
                    for j in range(NT):
                        nc.vector.tensor_scalar(x_ln[:, j, :], x_ln[:, j, :], mean_var[:, j, 0:1],
                                                rstd[:, j:j + 1], ALU.subtract, ALU.mult
                                                ).then_inc(z_made, 1)

                def split_y(b, par):
                    dve.wait_ge(y_hi_made, b + 1)
                    nc.vector.tensor_tensor(y_lo[:, par, :, :], y[:, :, :],
                                            y_hi[:, par, :, :].bitcast(F32), ALU.subtract
                                            ).then_inc(y_lo_made, 1)

                def split_g(b, m):
                    dve.wait_ge(g_hi_made, M * b + m + 1)
                    nc.vector.tensor_tensor(g_lo[:, m % RING, :, :], g[:, m % 2, :, :],
                                            g_hi[:, m % RING, :, :].bitcast(F32), ALU.subtract
                                            ).then_inc(g_lo_made, 1)

                def add_res(b, par):
                    dve.wait_ge(res_biased, b + 1)
                    dve.wait_ge(o_added, M * b + M)
                    for j in range(NT):
                        nc.vector.tensor_tensor(x_res[:, j, :], ps_o[:, par, j, :], x_res[:, j, :],
                                                ALU.add).then_inc(x_made, 1)

                norm_stats(0)
                normalise(0)
                for c in range(4):
                    split_w(c)
                split_y(0, 0)

                def step(b, par, first=False, last=False):
                    for m in range(M):
                        split_g(b, m)
                        if first and m < 4:
                            split_w(4 + m)
                        if m == 1 and not first:
                            add_res(b - 1, 1 - par)
                        if m == 2 and not last:
                            norm_stats(b + 1)
                        if m == 4 and not last:
                            normalise(b + 1)
                        if m == 6 and not last:
                            split_y(b + 1, 1 - par)

                step(0, 0, first=True)
                with dve.Fori(0, (B - 2) // 2) as i:
                    step(2 * i + 1, 1)
                    step(2 * i + 2, 0)
                step(B - 1, 1, last=True)
                add_res(B - 1, 1)

            @block.tensor
            def _(pe):
                def turn_x(b):
                    pe.wait_ge(z_made, NT * b + NT)
                    for i in range(2):
                        for k in (2 * i, 2 * i + 1):
                            for j in range(NT):
                                ins = nc.tensor.transpose(ps_x[:, k, j * P:j * P + P],
                                                          x_ln[:, j, k * P:k * P + P], ident[:, :])
                        ins.then_inc(turned, 1)

                def hidden(b, m, par, first=False):
                    if m == 0:
                        pe.wait_ge(y_lo_made, b + 1)
                    if not (first and m < 2):
                        pe.wait_ge(g_made, 2 * (M * b + m - 1))
                    for i in range(2):
                        col = (2 * m + i) * P
                        n = 0
                        for k in range(KT):
                            for w, a in ((w1_hi, y_hi), (w1_lo, y_hi), (w1_hi, y_lo)):
                                ins = nc.tensor.matmul(ps_h[:, m % 2, i, :], w[:, k, col:col + P],
                                                       a[:, par, k, :], start=(n == 0),
                                                       stop=(n == 3 * KT - 1))
                                n += 1
                    ins.then_inc(h_summed, 1)

                def output(b, m, par, first=False):
                    pe.wait_ge(g_lo_made, M * b + m + 1)
                    if m == 0 and not first:
                        pe.wait_ge(x_made, NT * (b - 1))
                    for j in range(NT):
                        n = 0
                        for i in range(2):
                            for a, w in ((g_hi, w2_hi), (g_lo, w2_hi), (g_hi, w2_lo)):
                                ins = nc.tensor.matmul(ps_o[:, par, j, :],
                                                       a[:, m % RING, i, j * P:j * P + P],
                                                       w[:, 2 * m + i, :], start=(m == 0 and n == 0),
                                                       stop=(m == M - 1 and n == 5))
                                n += 1
                    ins.then_inc(o_added, 1)

                pe.wait_ge(ident_made, 3)
                turn_x(0)
                pe.wait_ge(w_lo_made, 4)

                def step(b, par, first=False, second=False, last=False):
                    for m in range(M):
                        hidden(b, m, par, first)
                        if m >= LAG:
                            if first and m % 2 == 0:
                                pe.wait_ge(w_lo_made, 4 + m // 2)
                            output(b, m - LAG, par, first or second)
                        elif not first:
                            output(b - 1, m + M - LAG, 1 - par)
                        if m == 4 and not last:
                            pe.wait_ge(y_made, KT * b + KT)
                            turn_x(b + 1)

                step(0, 0, first=True)
                pe.wait_ge(w_lo_made, WCHUNKS)
                step(1, 1, second=True)
                with pe.Fori(1, (B - 2) // 2) as i:
                    step(2 * i, 0)
                    step(2 * i + 1, 1)
                step(B - 2, 0)
                step(B - 1, 1, last=True)
                for m in range(M - LAG, M):
                    output(B - 1, m, 1)

        nc.clear_and_free_semaphores(sems)
        nc.all_engine_barrier()


def style_phase(nc, x_in, context, keep, out, wq, wk, wv, b_stack, minus_lo, bv):
    name = "style"
    C, T = S, H
    CT = C // P
    TB = T // P
    D = C // NH
    HT = P // D
    ROW_MASK, ROW_MAX = 3 * D, 3 * D + 1
    ROWS = P // 2
    NB = NH // 2
    GROUPS = NH // 4
    HG = 2 * GROUPS
    BANKS = 4
    EXP_AND_LN = "natural_log_exp_and_others"
    SCALE = D ** -0.5
    BIG = 1e30
    NCONST = 3
    ROW_DMAS = HT
    OUT_DMAS = 8
    EXTRAS = [[] for _ in range(NH)]
    EXTRAS[3].append(("max", 1))
    for g_ in range(GROUPS):
        EXTRAS[4 * g_ + 3] += [("q", 2 * g_), ("k", 2 * g_)]
        EXTRAS[(4 * g_ + 4) % NH].append(("q", 2 * g_ + 1))
        EXTRAS[(4 * g_ + 5) % NH].append(("k", 2 * g_ + 1))
    EXTRAS[12].append(("max", 0))
    EXTRAS[10].append(("v", 0))
    EXTRAS[14].append(("v", 1))
    TURNS = 4 * NH + sum(len(e) for e in EXTRAS)

    def index(s, t):
        return sum(4 + len(e) for e in EXTRAS[:s]) + t

    SKIP = index(3, 5)

    def turn(b, s, t):
        return TURNS * (b + 1) + index(s, t) - SKIP

    def bank(s, t):
        return (index(s, t) - SKIP) % BANKS

    def extra(kind, j):
        return next((s, 4 + e.index((kind, j))) for s, e in enumerate(EXTRAS) if (kind, j) in e)

    def extra_turns(s, before=False, tail=0):
        return [(4 + e, kind, j) for e, (kind, j) in enumerate(EXTRAS[s])
                if not (before and index(s, 4 + e) < SKIP)
                and not (tail == 2 and (s > 3 or (s == 3 and kind != "max")))]

    with ExitStack() as ctx:
        sems = []

        def sb(n, shape, dtype=F32):
            return ctx.enter_context(nc.sbuf_tensor(f"{name}_{n}", shape, dtype))

        def pb(n, shape):
            return ctx.enter_context(nc.psum_tensor(f"{name}_{n}", shape, F32))

        def sem(n):
            sems.append(nc.alloc_semaphore(f"{name}_{n}"))
            return sems[-1]

        w_nat = sb("w_nat", [P, 3, CT, C])
        w_hi = sb("w_hi", [P, 2 * CT, NB, P], F32R)
        w_lo = sb("w_lo", [P, 2 * CT, NB, P], F32R)
        wv_hi = sb("wv_hi", [P, CT, C], F32R)
        wv_lo = sb("wv_lo", [P, CT, C], F32R)
        bias = sb("bias", [P, 2, NB])
        minus = sb("minus", [P, 2])
        minus_bias = sb("minus_bias", [P, 2, NB])
        bv_row = sb("bv_row", [P, C])
        ident = sb("ident", [P, P])
        mask_sel = sb("mask_sel", [1, P], F32R)
        minus_odd = sb("minus_odd", [2 * HT, 1])
        ones = sb("ones", [P, 2 * D])
        neg_half = sb("neg_half", [P, CT])
        xc = sb("xc", [P, 2, CT, T])
        xc_hi = sb("xc_hi", [P, 2, CT, T], F32R)
        xc_lo = sb("xc_lo", [P, 2, CT, T], F32R)
        neg_hi = sb("neg_hi", [P, 2, T], F32R)
        q_stack = sb("q_stack", [P, NB, T], F32R)
        k_stack = sb("k_stack", [P, NB, T], F32R)
        vv = sb("vv", [P, 2, TB, NH, 2 * D])
        keep_u8 = sb("keep_u8", [1, T], U8)
        key_row = sb("key_row", [1, T], F32R)
        mx = sb("mx", [P, TB, HT])
        mx2 = sb("mx2", [P, TB, 2 * HT])
        max_hi = sb("max_hi", [2 * HT, T], F32R)
        max_row = sb("max_row", [2 * HT, T], F32R)
        probs = sb("probs", [P, 2, 4, 2, T])
        den = sb("den", [P, T])
        raw = sb("raw", [P, T])
        rough = sb("rough", [P, T])
        newton = sb("newton", [P, T])
        moments = sb("moments", [P, 2, T])
        mean = sb("mean", [P, 2, CT, T])
        second = sb("second", [P, 2, CT, T])
        xf = sb("xf", [P, CT, T])
        work = sb("work", [P, CT, T])
        keep_b8 = sb("keep_b8", [P, T], U8)
        keep_b = sb("keep_b", [P, T])
        junk = sb("junk", [P, T])
        sum_x = sb("sum_x", [P, CT])
        sum_xx = sb("sum_xx", [P, CT])
        count = sb("count", [P, 1])
        small = sb("small", [P, 6, CT])
        MEAN, SEC, SQ, VAR, RSTD, RCNT = range(6)

        ps_a = pb("ps_a", [P, BANKS, T])
        ps_s = pb("ps_s", [P, 2, T])
        ps_m = pb("ps_m", [P, T])
        ps_d = pb("ps_d", [P, T])

        (consts_loaded, weights_loaded, w_hi_made, w_lo_made, ident_made, odd_made, ones_made,
         w_cleared, minus_bias_made, sel_made) = (
             sem(n) for n in ("consts_loaded", "weights_loaded", "w_hi_made", "w_lo_made",
                              "ident_made", "odd_made", "ones_made", "w_cleared",
                              "minus_bias_made", "sel_made"))
        xc_loaded, xc_hi_made, xc_lo_made = sem("xc_loaded"), sem("xc_hi_made"), sem("xc_lo_made")
        keep_loaded, key_made = sem("keep_loaded"), sem("key_made")
        turn_filled, turn_read = sem("turn_filled"), sem("turn_read")
        neg_hi_made, v_made, vv_made = sem("neg_hi_made"), sem("v_made"), sem("vv_made")
        mx2_made, max_hi_made, max_made = sem("mx2_made"), sem("max_hi_made"), sem("max_made")
        max_placed = [sem(f"max_placed{i}") for i in range(2)]
        rescored, exped, weighed = sem("rescored"), sem("exped"), sem("weighed")
        den_copied, raw_copied = sem("den_copied"), sem("raw_copied")
        log_made, rough_made = sem("log_made"), sem("rough_made")
        newton_made, refined, moments_made = sem("newton_made"), sem("refined"), sem("moments_made")
        moments_moved = [sem(f"moments_moved{i}") for i in range(2)]
        xf_loaded, keep_b_loaded, keep_b_made = sem("xf_loaded"), sem("keep_b_loaded"), sem("keep_b_made")
        x_kept, summed, counted = sem("x_kept"), sem("summed"), sem("counted")
        count_made = sem("count_made")
        small_made, rstd_made, x_normed = sem("small_made"), sem("rstd_made"), sem("x_normed")
        squared, var_made, clipped, rooted = sem("squared"), sem("var_made"), sem("clipped"), sem("rooted")
        styled, shifted, finished, stored = sem("styled"), sem("shifted"), sem("finished"), sem("stored")
        SMALL = 5

        out_v = out.rearrange("b (j p) d -> b p j d", p=P)
        x_v = x_in.rearrange("b (j p) d -> b p j d", p=P)
        c_v = context.rearrange("b (j p) d -> b p j d", p=P)

        with nc.Block() as block:

            @block.sync
            def _(sp):
                def load_xc(b):
                    sp.dma_start(xc[:, 0, :, :], x_v[b]).then_inc(xc_loaded, DMA)
                    sp.dma_start(xc[:, 1, :, :], c_v[b]).then_inc(xc_loaded, DMA)

                def load_keep(b):
                    sp.dma_start(keep_u8[:, :], keep[b]).then_inc(keep_loaded, DMA)

                def place_max(b, half):
                    sp.wait_ge(max_made, 2 * b + half + 1)
                    for h in range(HT):
                        row = 64 * (h % 2) + ROW_MAX
                        sp.dma_start(q_stack[row:row + 2, 4 * half + h // 2, :].bitcast(F32),
                                     max_row[2 * h:2 * h + 2, :].bitcast(F32)
                                     ).then_inc(max_placed[half], DMA)

                def load_final(b):
                    sp.dma_start(xf[:, :, :], x_v[b]).then_inc(xf_loaded, DMA)
                    sp.dma_start(keep_b8[:, :], keep[b].broadcast_to([P, T])).then_inc(keep_b_loaded, DMA)

                def store(b):
                    sp.wait_ge(finished, b + 1)
                    sp.dma_start(out_v[b], xf[:, :, :]).then_inc(stored, DMA)

                for i, w in enumerate((wq, wk, wv)):
                    sp.dma_start(w_nat[:, i, :, :], w.rearrange("(k p) n -> p k n", p=P)
                                 ).then_inc(weights_loaded, DMA)
                load_xc(0)
                load_keep(0)
                sp.dma_start(bias[:, :, :], b_stack).then_inc(consts_loaded, DMA)
                sp.dma_start(minus[:, :], minus_lo).then_inc(consts_loaded, DMA)
                sp.dma_start(bv_row[:, :], bv.broadcast_to([P, C])).then_inc(consts_loaded, DMA)
                load_final(0)

                def step(b, first=False, tail=0):
                    if tail < 2:
                        sp.wait_ge(xc_lo_made, 2 * (b + 2))
                        sp.wait_ge(key_made, b + 2)
                        if tail < 1:
                            load_xc(b + 2)
                            load_keep(b + 2)
                    if not (isinstance(b, int) and b < 0):
                        place_max(b, 1)
                    if tail < 2:
                        place_max(b + 1, 0)
                    if not (first or isinstance(b, int) and b < 0):
                        store(b - 1)
                        sp.wait_ge(stored, DMA * b)
                        load_final(b)

                step(-1)
                step(0, first=True)
                with sp.Fori(1, B - 2) as b:
                    step(b)
                step(B - 2, tail=1)
                step(B - 1, tail=2)
                store(B - 1)
                sp.wait_ge(stored, DMA * B)

            @block.gpsimd
            def _(pool):
                for w in (w_hi, w_lo):
                    rows = w[:, :, :, :].rearrange("p i j (e r) -> p (i j e) r", e=2)
                    nc.gpsimd.memset(rows[:, :, 3 * D:].bitcast(F32), 0.0).then_inc(w_cleared, 1)
                nc.gpsimd.memset(ident[:, :], 0.0).then_inc(ident_made, 1)
                nc.gpsimd.memset(neg_half[:, :], -0.5).then_inc(ident_made, 1)
                pool.wait_ge(ident_made, 2)
                nc.gpsimd.affine_select(out=ident[:, :], in_=ident[:, :], compare_op=ALU.not_equal,
                                        fill=1.0, base=0, pattern=[[-1, P]], channel_multiplier=1
                                        ).then_inc(ident_made, 1)
                nc.gpsimd.memset(ones[:, :], 1.0).then_inc(ones_made, 1)
                nc.gpsimd.memset(mask_sel[:, :].bitcast(F32), 0.0).then_inc(sel_made, 1)
                pool.wait_ge(sel_made, 1)
                nc.gpsimd.memset(mask_sel[:, ROW_MASK::64].bitcast(F32), 1.0).then_inc(sel_made, 1)

                def round_xc(b, first=False):
                    n_xc_loaded = counted_to(pool, 2 * DMA * (b + 1))
                    n_turns = counted_to(pool, turn(b - 1, *extra("k", NB - 1)) + 1)
                    pool.wait_ge(ident_made, 1)
                    pool.wait_ge(xc_loaded, n_xc_loaded)
                    if not first:
                        pool.wait_ge(turn_filled, n_turns)
                    for i in range(2):
                        nc.gpsimd.tensor_scalar(xc_hi[:, i, :, :], xc[:, i, :, :], 1.0, 0.0,
                                                ALU.mult, ALU.add).then_inc(xc_hi_made, 1)

                def square_v(b, par):
                    pool.wait_ge(v_made, 2 * b + 2)
                    v = vv[:, par, :, :, 0:D].rearrange("p t h d -> p (t h) d")
                    nc.gpsimd.tensor_tensor(vv[:, par, :, :, D:2 * D].rearrange("p t h d -> p (t h) d"),
                                            v, v, ALU.mult).then_inc(vv_made, 1)

                def move_moments(b, par, g):
                    n_moments_made = counted_to(pool, GROUPS * b + g + 1)
                    pool.wait_ge(ident_made, 1)
                    pool.wait_ge(moments_made, n_moments_made)
                    for h in range(4):
                        for i, dst in enumerate((mean, second)):
                            row = D * ((4 * g + h) % HT)
                            src = 2 * D * h + D * i
                            pool.dma_start(dst[row:row + D, par, g // 2, :],
                                           moments[src:src + D, g % 2, :]
                                           ).then_inc(moments_moved[g % 2], DMA)

                def keep_x(b, first=False):
                    n_keep_b_loaded = counted_to(pool, DMA * (b + 1))
                    n_finished = counted_to(pool, b)
                    pool.wait_ge(ident_made, 1)
                    pool.wait_ge(keep_b_loaded, n_keep_b_loaded)
                    if not first:
                        pool.wait_ge(finished, n_finished)
                    nc.gpsimd.tensor_scalar(keep_b[:, :], keep_b8[:, :], 1.0, 0.0, ALU.mult, ALU.add
                                            ).then_inc(keep_b_made, 1)
                    pool.wait_ge(keep_b_made, b + 1)
                    pool.wait_ge(xf_loaded, DMA * (b + 1))
                    nc.gpsimd.tensor_tensor(xf[:, :, :], xf[:, :, :],
                                            keep_b[:, :].unsqueeze(1).to_broadcast([P, CT, T]), ALU.mult
                                            ).then_inc(x_kept, 1)

                def instance_stats(b):
                    pool.wait_ge(counted, b + 1)
                    pool.wait_ge(summed, 4 * (b + 1))
                    rc = small[:, RCNT, 0:1].to_broadcast([P, CT])
                    nc.gpsimd.tensor_tensor(small[:, MEAN, :], sum_x[:, :], rc, ALU.mult).then_inc(small_made, 1)
                    nc.gpsimd.tensor_tensor(small[:, SEC, :], sum_xx[:, :], rc, ALU.mult).then_inc(small_made, 1)
                    pool.wait_ge(small_made, SMALL * b + 2)
                    nc.gpsimd.tensor_tensor(small[:, SQ, :], small[:, MEAN, :], small[:, MEAN, :], ALU.mult
                                            ).then_inc(small_made, 1)
                    pool.wait_ge(small_made, SMALL * b + 3)
                    nc.gpsimd.tensor_tensor(small[:, VAR, :], small[:, SEC, :], small[:, SQ, :], ALU.subtract
                                            ).then_inc(small_made, 1)
                    n_small_made = counted_to(pool, SMALL * b + 4)
                    pool.wait_ge(ident_made, 1)
                    pool.wait_ge(small_made, n_small_made)
                    nc.gpsimd.tensor_scalar(small[:, VAR, :], small[:, VAR, :], 0.0, EPS, ALU.max, ALU.add
                                            ).then_inc(small_made, 1)
                    pool.wait_ge(small_made, SMALL * b + 5)
                    nc.gpsimd.tensor_tensor(small[:, RSTD, :], small[:, VAR, :], neg_half[:, :], ALU.pow
                                            ).then_inc(rstd_made, 1)

                def put_together(b, par):
                    pool.wait_ge(x_normed, CT * (b + 1))
                    pool.wait_ge(rooted, b + 1)
                    nc.gpsimd.tensor_tensor(xf[:, :, :], xf[:, :, :], work[:, :, :], ALU.mult
                                            ).then_inc(styled, 1)
                    pool.wait_ge(styled, b + 1)
                    nc.gpsimd.tensor_tensor(xf[:, :, :], xf[:, :, :], mean[:, par, :, :], ALU.add
                                            ).then_inc(shifted, 1)

                def step(b, par, first=False, second=False, tail=0):
                    if tail < 2:
                        round_xc(b + 1)
                    if not first:
                        move_moments(b - 1, 1 - par, GROUPS - 1)
                        keep_x(b - 1, second)
                        instance_stats(b - 1)
                    move_moments(b, par, 0)
                    move_moments(b, par, 1)
                    if not first:
                        put_together(b - 1, 1 - par)
                    if tail < 2:
                        square_v(b + 1, 1 - par)
                    move_moments(b, par, 2)

                round_xc(0, True)
                square_v(0, 0)
                step(0, 0, first=True)
                step(1, 1, second=True)
                with pool.Fori(1, (B - 2) // 2) as i:
                    step(2 * i, 0)
                    step(2 * i + 1, 1)
                step(B - 2, 0, tail=1)
                step(B - 1, 1, tail=2)
                move_moments(B - 1, 1, GROUPS - 1)
                keep_x(B - 1)
                instance_stats(B - 1)
                put_together(B - 1, 1)

            @block.scalar
            def _(act):
                def negate_hi(b, s, t, kind, j):
                    act.wait_ge(turn_filled, turn(b, s, t) + 1)
                    nc.scalar.activation(neg_hi[:, kind, :], ps_a[:, bank(s, t), :], ACT.Identity,
                                         scale=minus[:, kind:kind + 1], bias=minus_bias[:, kind, j:j + 1]
                                         ).then_inc(neg_hi_made, 1)

                def copy_max(b, s, t):
                    act.wait_ge(turn_filled, turn(b, s, t) + 1)
                    nc.scalar.activation(max_hi[:, :], ps_a[0:2 * HT, bank(s, t), :], ACT.Copy
                                         ).then_inc(max_hi_made, 1)

                def extras(b, s, before=False, tail=0):
                    for e, kind, j in extra_turns(s, before, tail):
                        if kind in ("q", "k"):
                            negate_hi(b, s, e, int(kind == "k"), j)
                        elif kind == "max":
                            copy_max(b, s, e)

                def exp_unit(b, u, first=False):
                    hg, h, i = u // 8, u // 2 % 4, u % 2
                    act.wait_ge(rescored, 8 * HG * b + u + 1)
                    if u % 8 == 0 and not (first and hg < 2):
                        act.wait_ge(weighed, HG * b + hg - 1)
                    nc.scalar.activation(probs[:, hg % 2, h, i, :], ps_s[:, i, :], ACT.Exp,
                                         scale=SCALE).then_inc(exped, 1)

                def copy_den(b, g, first=False):
                    act.wait_ge(weighed, HG * b + 2 * g + 2)
                    if not (first and g == 0):
                        act.wait_ge(refined, GROUPS * b + g)
                    nc.scalar.activation(den[:, :], ps_d[:, :], ACT.Copy).then_inc(den_copied, 1)

                def rough_recip(b, g):
                    act.wait_ge(den_copied, GROUPS * b + g + 1)
                    nc.scalar.activation(rough[:, :], den[:, :], ACT.Ln).then_inc(log_made, 1)
                    act.wait_ge(log_made, GROUPS * b + g + 1)
                    nc.scalar.activation(rough[:, :], rough[:, :], ACT.Exp, scale=-1.0).then_inc(rough_made, 1)

                def sums(b, first=False):
                    act.wait_ge(x_kept, b + 1)
                    for t in range(CT):
                        for f, acc in ((ACT.Copy, sum_x), (ACT.Square, sum_xx)):
                            if not (first and t == 0 and f == ACT.Copy):
                                act.wait_ge(summed, 4 * b + 2 * t + (f == ACT.Square))
                            nc.scalar.activation(junk[:, :], xf[:, t, :], f, accum_out=acc[:, t:t + 1]
                                                 ).then_inc(summed, 1)

                def square_mean(b, par):
                    act.wait_ge(moments_moved[0], 2 * OUT_DMAS * DMA * (b + 1))
                    act.wait_ge(moments_moved[1], 2 * OUT_DMAS * DMA * (b + 1))
                    nc.scalar.activation(work[:, :, :], mean[:, par, :, :], ACT.Square).then_inc(squared, 1)

                def root(b):
                    act.wait_ge(clipped, b + 1)
                    nc.scalar.activation(work[:, :, :], work[:, :, :], ACT.Sqrt).then_inc(rooted, 1)
                    nc.scalar.preload_act_table_set(EXP_AND_LN)

                nc.scalar.preload_act_table_set(EXP_AND_LN)
                act.wait_ge(minus_bias_made, 2)
                for s in range(3, NH):
                    extras(-1, s, before=True)

                def step(b, par, first=False, tail=0, second=False):
                    for s in range(NH):
                        for u in range(4 * s, 4 * s + 4):
                            exp_unit(b, u, first)
                            if u % 4 == 2 and s == 1 and not first:
                                copy_den(b - 1, GROUPS - 1)
                            if u % 4 == 2 and s in (5, 9, 13):
                                copy_den(b, (s - 5) // 4, first)
                        extras(b, s, tail=tail)
                        if s == 1 and not first:
                            rough_recip(b - 1, GROUPS - 1)
                        if s in (5, 9, 13):
                            rough_recip(b, (s - 5) // 4)
                        if not first:
                            if s == 4:
                                sums(b - 1, second)
                            if s == 7:
                                square_mean(b - 1, 1 - par)
                            if s == 11:
                                root(b - 1)

                step(0, 0, first=True)
                step(1, 1, second=True)
                with act.Fori(1, (B - 2) // 2) as i:
                    step(2 * i, 0)
                    step(2 * i + 1, 1)
                step(B - 2, 0, tail=1)
                step(B - 1, 1, tail=2)
                copy_den(B - 1, GROUPS - 1)
                rough_recip(B - 1, GROUPS - 1)
                sums(B - 1)
                square_mean(B - 1, 1)
                root(B - 1)

            @block.vector
            def _(dve):
                def split_xc(b):
                    for i in range(2):
                        dve.wait_ge(xc_hi_made, 2 * b + i + 1)
                        nc.vector.tensor_tensor(xc_lo[:, i, :, :], xc[:, i, :, :],
                                                xc_hi[:, i, :, :].bitcast(F32), ALU.subtract
                                                ).then_inc(xc_lo_made, 1)

                def key_mask(b):
                    dve.wait_ge(keep_loaded, DMA * (b + 1))
                    nc.vector.tensor_scalar(key_row[:, :], keep_u8[:, :], BIG, -BIG, ALU.mult, ALU.add
                                            ).then_inc(key_made, 1)

                def stack(b, s, t, kind, j, first=False):
                    order = [("qk".index(k), jj) for ss in (*range(3, NH), *range(3))
                             for k, jj in EXTRAS[ss] if k in ("q", "k")]
                    n = 2 * NB * (b + (1 if s >= 3 else 0)) + order.index((kind, j)) + 1
                    dve.wait_ge(neg_hi_made, n)
                    if not first:
                        done = 8 * HG * (b if s >= 3 else b - 1) + 16 * (j // 2 + 1)
                        dve.wait_ge(rescored, done)
                    nc.vector.scalar_tensor_tensor(
                        out=(q_stack, k_stack)[kind][:, j, :], in0=ps_a[:, bank(s, t), :],
                        scalar=bias[:, kind, j:j + 1], in1=neg_hi[:, kind, :].bitcast(F32),
                        op0=ALU.add, op1=ALU.add).then_inc(turn_read, 1)

                def bias_v_rows(b, par, s, t, i, first=False):
                    if i == 0 and not first:
                        dve.wait_ge(weighed, HG * b)
                    dve.wait_ge(turn_filled, turn(b, s, t) + 1)
                    nc.vector.tensor_tensor(
                        vv[:, 1 - par, 2 * i:2 * i + 2, :, 0:D],
                        ps_a[:, bank(s, t), :].rearrange("p (t h d) -> p t h d", t=2, d=D),
                        bv_row[:, :].rearrange("p (h d) -> p h d", d=D).unsqueeze(1)
                        .to_broadcast([P, 2, NH, D]), ALU.add).then_inc(v_made, 1)
                    dve.wait_ge(v_made, 2 * (b + 1) + i + 1)
                    dve.sem_inc(turn_read, 1)

                def maxima(b, s, tiles, first=False):
                    h = (s - 4) % HT
                    for t in tiles:
                        dve.wait_ge(turn_filled, turn(b, s, t) + 1)
                        if h == 0 and t == 0 and not first:
                            half = 0 if s == 4 else 1
                            dve.wait_ge(mx2_made, 2 * b + 2 + half)
                        nc.vector.tensor_reduce(mx[:, t, h:h + 1], ps_a[:, bank(s, t), :],
                                                axis=AX.X, op=ALU.max).then_inc(turn_read, 1)

                def double_max(b, s, half, first=False):
                    dve.wait_ge(turn_read, turn(b, s, TB - 1) + 1)
                    if not first:
                        k, kk = extra("max", 1 - half)
                        dve.wait_ge(turn_filled, turn(b if half == 0 else b - 1, k, kk) + 1)
                    nc.vector.tensor_scalar(
                        mx2[:, :, :].rearrange("p t (h e) -> p (t h) e", e=2),
                        mx[:, :, :].rearrange("p t h -> p (t h)").unsqueeze(2)
                        .to_broadcast([P, TB * HT, 2]), -1.0, None, ALU.mult).then_inc(mx2_made, 1)

                def split_max(b, s, t, half, first=False):
                    n = b + 1 - half
                    dve.wait_ge(max_hi_made, 2 * n + half + 1)
                    if half == 1:
                        dve.wait_ge(max_placed[0], ROW_DMAS * DMA * (n + 1))
                    elif not first:
                        dve.wait_ge(max_placed[1], ROW_DMAS * DMA * n)
                    nc.vector.scalar_tensor_tensor(
                        out=max_row[:, :], in0=max_hi[:, :].bitcast(F32), scalar=minus_odd[:, 0:1],
                        in1=ps_a[0:2 * HT, bank(s, t), :], op0=ALU.mult, op1=ALU.add
                        ).then_inc(max_made, 1)
                    dve.wait_ge(max_made, 2 * n + half + 1)
                    dve.sem_inc(turn_read, 1)

                def extras(b, par, s, first=False, before=False, tail=0):
                    for e, kind, j in extra_turns(s, before, tail):
                        if kind in ("q", "k"):
                            stack(b, s, e, int(kind == "k"), j, first)
                        elif kind == "v":
                            bias_v_rows(b, par, s, e, j, first)
                        else:
                            split_max(b, s, e, j, first)

                def copy_raw(b, g, first=False):
                    dve.wait_ge(weighed, HG * b + 2 * g + 2)
                    if not (first and g == 0):
                        dve.wait_ge(moments_made, GROUPS * b + g)
                    nc.vector.tensor_copy(raw[:, :], ps_m[:, :]).then_inc(raw_copied, 1)

                def refine(b, g):
                    n = GROUPS * b + g + 1
                    dve.wait_ge(rough_made, n)
                    nc.vector.tensor_tensor(newton[:, :], den[:, :], rough[:, :], ALU.mult
                                            ).then_inc(newton_made, 1)
                    dve.wait_ge(newton_made, n)
                    nc.vector.scalar_tensor_tensor(out=newton[:, :], in0=newton[:, :], scalar=-2.0,
                                                   in1=rough[:, :], op0=ALU.add, op1=ALU.mult
                                                   ).then_inc(refined, 1)

                def make_moments(b, g, first=False):
                    dve.wait_ge(refined, GROUPS * b + g + 1)
                    if not (first and g < 2):
                        k = 2 * b + g // 2
                        dve.wait_ge(moments_moved[g % 2], OUT_DMAS * DMA * k)
                    nc.vector.scalar_tensor_tensor(out=moments[:, g % 2, :], in0=newton[:, :], scalar=-1.0,
                                                   in1=raw[:, :], op0=ALU.mult, op1=ALU.mult
                                                   ).then_inc(moments_made, 1)

                def recip_count(b, first=False):
                    dve.wait_ge(keep_b_made, b + 1)
                    if not first:
                        dve.wait_ge(rstd_made, b)
                    nc.vector.tensor_reduce(count[:, :], keep_b[:, :], axis=AX.X, op=ALU.add
                                            ).then_inc(count_made, 1)
                    dve.wait_ge(count_made, b + 1)
                    nc.vector.reciprocal(small[:, RCNT, 0:1], count[:, :]).then_inc(counted, 1)

                def normalise(b):
                    dve.wait_ge(rstd_made, b + 1)
                    dve.wait_ge(summed, 4 * (b + 1))
                    for t in range(CT):
                        nc.vector.tensor_scalar(xf[:, t, :], xf[:, t, :], small[:, MEAN, t:t + 1],
                                                small[:, RSTD, t:t + 1], ALU.subtract, ALU.mult
                                                ).then_inc(x_normed, 1)

                def variance(b, par):
                    dve.wait_ge(squared, b + 1)
                    nc.vector.tensor_tensor(work[:, :, :], second[:, par, :, :], work[:, :, :], ALU.subtract
                                            ).then_inc(var_made, 1)
                    dve.wait_ge(var_made, b + 1)
                    nc.vector.tensor_scalar(work[:, :, :], work[:, :, :], 0.0, None, ALU.max
                                            ).then_inc(clipped, 1)

                def finish(b):
                    dve.wait_ge(shifted, b + 1)
                    nc.vector.tensor_tensor(xf[:, :, :], xf[:, :, :],
                                            keep_b[:, :].unsqueeze(1).to_broadcast([P, CT, T]), ALU.mult
                                            ).then_inc(finished, 1)

                dve.wait_ge(consts_loaded, DMA * NCONST)
                for kind in range(2):
                    nc.vector.tensor_scalar(minus_bias[:, kind, :], bias[:, kind, :],
                                            minus[:, kind:kind + 1], None, ALU.mult
                                            ).then_inc(minus_bias_made, 1)
                dve.wait_ge(weights_loaded, 3 * DMA)
                dve.wait_ge(w_cleared, 2)
                from_nat = w_nat[:, 0:2, :, :].rearrange("p i k (h d) -> p (i k h) d", d=D)
                hi_rows = w_hi[:, :, :, :].rearrange("p i j (e r) -> p (i j e) r", e=2)
                lo_rows = w_lo[:, :, :, :].rearrange("p i j (e r) -> p (i j e) r", e=2)
                for r in range(3):
                    nc.vector.tensor_copy(hi_rows[:, :, D * r:D * r + D], from_nat).then_inc(w_hi_made, 1)
                nc.vector.tensor_copy(wv_hi[:, :, :], w_nat[:, 2, :, :]).then_inc(w_hi_made, 1)
                for r in range(3):
                    dve.wait_ge(w_hi_made, r + 1)
                    nc.vector.tensor_tensor(lo_rows[:, :, D * r:D * r + D], from_nat,
                                            hi_rows[:, :, D * r:D * r + D].bitcast(F32), ALU.subtract
                                            ).then_inc(w_lo_made, 1)
                dve.wait_ge(w_hi_made, 4)
                nc.vector.tensor_tensor(wv_lo[:, :, :], w_nat[:, 2, :, :],
                                        wv_hi[:, :, :].bitcast(F32), ALU.subtract).then_inc(w_lo_made, 1)
                dve.wait_ge(ident_made, 3)
                nc.vector.tensor_reduce(minus_odd[:, :], ident[0:2 * HT, 1:2 * HT:2], axis=AX.X,
                                        op=ALU.add, negate=True).then_inc(odd_made, 1)
                split_xc(0)
                key_mask(0)
                dve.wait_ge(odd_made, 1)
                for s in range(3, NH):
                    if s >= 4:
                        maxima(-1, s, range(TB), s == 4)
                    if s == 11:
                        double_max(-1, 11, 0, True)
                    extras(-1, 1, s, True, before=True)

                def step(b, par, first=False, tail=0, second=False):
                    for s in range(NH):
                        if s == 2:
                            if tail < 2:
                                split_xc(b + 1)
                                key_mask(b + 1)
                        if tail < 2 or s < 4:
                            maxima(b, s, range(0, 2))
                        if s == 2 and not first:
                            refine(b - 1, GROUPS - 1)
                        if s == 3 and not first:
                            make_moments(b - 1, GROUPS - 1)
                        if s in (6, 10, 14):
                            refine(b, (s - 6) // 4)
                        if s in (7, 11, 15):
                            make_moments(b, (s - 7) // 4, first)
                        if tail < 2 or s < 4:
                            maxima(b, s, range(2, 3))
                        if s == 1 and not first:
                            copy_raw(b - 1, GROUPS - 1)
                        if s in (5, 9, 13):
                            copy_raw(b, (s - 5) // 4, first)
                        if tail < 2 or s < 4:
                            maxima(b, s, range(3, 4))
                        if s == 3:
                            double_max(b, 3, 1)
                        if s == 11 and tail < 2:
                            double_max(b, 11, 0)
                        extras(b, par, s, first and s < 3, tail=tail)
                        if not first:
                            if s == 3:
                                recip_count(b - 1, second)
                            if s == 8:
                                normalise(b - 1)
                            if s == 9:
                                variance(b - 1, 1 - par)
                            if s == 14:
                                finish(b - 1)

                step(0, 0, first=True)
                step(1, 1, second=True)
                with dve.Fori(1, (B - 2) // 2) as i:
                    step(2 * i, 0)
                    step(2 * i + 1, 1)
                step(B - 2, 0, tail=1)
                step(B - 1, 1, tail=2)
                copy_raw(B - 1, GROUPS - 1)
                refine(B - 1, GROUPS - 1)
                make_moments(B - 1, GROUPS - 1)
                recip_count(B - 1)
                normalise(B - 1)
                variance(B - 1, 1)
                finish(B - 1)

            @block.tensor
            def _(pe):
                def wait_bank(b, s, t):
                    n = turn(b, s, t) - BANKS + 1
                    if not (isinstance(n, int) and n < 1):
                        pe.wait_ge(turn_read, n)

                def project(b, s, t, kind, j):
                    n = b + 1 if s >= 3 else b
                    if j == 0:
                        pe.wait_ge(xc_lo_made, 2 * n + kind + 1)
                        pe.wait_ge(key_made, n + 1)
                    wait_bank(b, s, t)
                    steps = [(w, a, k) for k in range(CT)
                             for w, a in ((w_hi, xc_hi), (w_lo, xc_hi), (w_hi, xc_lo))]
                    for m, (w, a, k) in enumerate(steps):
                        ins = nc.tensor.matmul(ps_a[:, bank(s, t), :], w[:, CT * kind + k, j, :],
                                               a[:, kind, k, :], start=(m == 0),
                                               stop=(kind == 0 and m == len(steps) - 1))
                    if kind == 1:
                        ins = nc.tensor.matmul(ps_a[:, bank(s, t), :], mask_sel[:, :], key_row[:, :],
                                               start=False, stop=True)
                    ins.then_inc(turn_filled, 1)

                def project_v(b, s, t, i):
                    pe.wait_ge(xc_lo_made, 2 * (b + 1) + 2)
                    wait_bank(b, s, t)
                    for tile in range(2):
                        m = 0
                        col = (2 * i + tile) * P
                        for k in range(CT):
                            for a, w in ((xc_hi, wv_hi), (xc_lo, wv_hi), (xc_hi, wv_lo)):
                                ins = nc.tensor.matmul(ps_a[:, bank(s, t), tile * C:tile * C + C],
                                                       a[:, 1, k, col:col + P], w[:, k, :],
                                                       start=(m == 0), stop=(m == 3 * CT - 1))
                                m += 1
                    ins.then_inc(turn_filled, 1)

                def scores(b, s, tiles):
                    h = (s - 4) % NH
                    base = 64 * (h % 2)
                    for t in tiles:
                        if h % 4 == 0 and t == 0:
                            ks, kt = extra("k", h // 2)
                            pe.wait_ge(turn_read, turn(b if ks < s else b - 1, ks, kt) + 1)
                        if h % 4 == 2 and t == 0:
                            ks, kt = extra("k", h // 2)
                            pe.wait_ge(turn_read, turn(b, ks, kt) + 1)
                        wait_bank(b, s, t)
                        nc.tensor.matmul(ps_a[:, bank(s, t), :],
                                         q_stack[base:base + ROWS, h // 2, t * P:t * P + P],
                                         k_stack[base:base + ROWS, h // 2, :],
                                         start=True, stop=True).then_inc(turn_filled, 1)

                def turn_max(b, s, t, half):
                    pe.wait_ge(mx2_made, 2 * (b + 1 - half) + half + 1)
                    wait_bank(b, s, t)
                    for i in range(TB):
                        ins = nc.tensor.transpose(ps_a[0:2 * HT, bank(s, t), i * P:i * P + P],
                                                  mx2[:, i, :], ident[:, :])
                    ins.then_inc(turn_filled, 1)

                def extras(b, s, before=False, tail=0):
                    for e, kind, j in extra_turns(s, before, tail):
                        if kind in ("q", "k"):
                            project(b, s, e, int(kind == "k"), j)
                        elif kind == "v":
                            project_v(b, s, e, j)
                        else:
                            turn_max(b, s, e, j)

                def rescore(b, u, first=False):
                    hg, h, i = u // 8, u // 2 % 4, u % 2
                    head, col = 4 * (hg // 2) + h, (2 * (hg % 2) + i) * P
                    base = 64 * (head % 2)
                    if u % 32 == 0:
                        pe.wait_ge(max_placed[u // 32], ROW_DMAS * DMA * (b + 1))
                    if not (first and u < 2):
                        pe.wait_ge(exped, 8 * HG * b + u - 1)
                    nc.tensor.matmul(ps_s[:, i, :],
                                     k_stack[base:base + ROWS, head // 2, col:col + P],
                                     q_stack[base:base + ROWS, head // 2, :],
                                     start=True, stop=True).then_inc(rescored, 1)

                def weigh(b, hg, i, is_sum, par, first=False):
                    g, half = hg // 2, hg % 2
                    if i == 0 and not is_sum:
                        pe.wait_ge(exped, 8 * (HG * b + hg + 1))
                        if hg == 0:
                            pe.wait_ge(vv_made, b + 1)
                        if half == 0 and not (first and g == 0):
                            pe.wait_ge(den_copied, GROUPS * b + g)
                            pe.wait_ge(raw_copied, GROUPS * b + g)
                    for h in range(4):
                        lhs = ones[:, :] if is_sum else vv[:, par, 2 * half + i, 4 * g + h, :]
                        ins = nc.tensor.matmul((ps_m, ps_d)[is_sum][2 * D * h:2 * D * h + 2 * D, :],
                                               lhs, probs[:, hg % 2, h, i, :],
                                               start=(half == 0 and i == 0),
                                               stop=(half == 1 and i == 1))
                    if i == 1 and is_sum:
                        ins.then_inc(weighed, 1)

                pe.wait_ge(w_lo_made, 4)
                pe.wait_ge(ident_made, 3)
                pe.wait_ge(ones_made, 1)
                pe.wait_ge(sel_made, 2)
                for s in range(3, NH):
                    if s >= 4:
                        scores(-1, s, range(TB))
                    extras(-1, s, before=True)

                ORDERS = ("RWRW01R2R3", "R0WR1WR2R3", "R0R1W2R3WR")

                def step(b, par, first=False, tail=0):
                    for s in range(NH):
                        scored = tail < 2 or s < 4
                        n_r = n_w = 0

                        def weigh_part(is_sum):
                            if s >= 2:
                                weigh(b, (s - 2) // 2, s % 2, is_sum, par, first)
                            elif not first:
                                weigh(b - 1, HG - 1, s, is_sum, 1 - par)

                        for what in ORDERS[2 if s == 3 else s % 2]:
                            if what == "R":
                                rescore(b, 4 * s + n_r, first)
                                n_r += 1
                            elif what == "W":
                                weigh_part(n_w == 1)
                                n_w += 1
                            elif scored:
                                scores(b, s, [int(what)])
                        extras(b, s, tail=tail)

                step(0, 0, first=True)
                with pe.Fori(0, (B - 2) // 2) as i:
                    step(2 * i + 1, 1)
                    step(2 * i + 2, 0)
                step(B - 1, 1, tail=2)
                for i in range(2):
                    weigh(B - 1, HG - 1, i, False, 1)
                    weigh(B - 1, HG - 1, i, True, 1)

        nc.clear_and_free_semaphores(sems)
        nc.all_engine_barrier()


def program(nc, x, context, mask1, mask2, keep, ln1_s, ln1_b, w_qkv1, b_qk1, b_v1, w_o1, b_o1,
            ln2_s, ln2_b, w_qkv2, b_qk2, b_v2, w_o2, b_o2, ln3_s, ln3_b, w1, b1, w2, b2,
            wq, wk, wv, b_stack, minus_lo, bv, out):
    x1, x2, x3 = (nc.dram_tensor(n, [B, S, H], F32).ap() for n in ("x1", "x2", "x3"))
    attention_phase(nc, "self", False, x, x1, None, mask1, w_qkv1, w_o1, b_qk1, b_v1, b_o1, ln1_s, ln1_b)
    attention_phase(nc, "cross", True, x1, x2, context, mask2, w_qkv2, w_o2, b_qk2, b_v2, b_o2,
                    ln2_s, ln2_b)
    mlp_phase(nc, x2, x3, w1, w2, b1, b2, ln3_s, ln3_b)
    style_phase(nc, x3, context, keep, out, wq, wk, wv, b_stack, minus_lo, bv)


def laid_out(inputs):
    import numpy as np

    a = {k: np.asarray(v) for k, v in inputs.items()}
    l0 = {k[len("L0_xattn_"):]: v for k, v in a.items() if k.startswith("L0_xattn_")}
    l1 = {k[len("L1_xattn_"):]: v for k, v in a.items() if k.startswith("L1_xattn_")}

    def col(v):
        return v.reshape(-1, P).T

    def row(v):
        return v.reshape(1, -1)

    D1 = S // NH
    b_stack = np.zeros((2, NH // 2, 2, 64), np.float32)
    for kind, b in enumerate((l1["bq"], l1["bk"])):
        for r in range(3):
            b_stack[kind, :, :, D1 * r:D1 * r + D1] = b.reshape(NH // 2, 2, D1)
    b_stack[0, :, :, 3 * D1] = 1.0
    b_stack[1, :, :, 3 * D1 + 1:3 * D1 + 3] = 1.0
    b_stack = b_stack.reshape(2, NH // 2, P).transpose(2, 0, 1)
    minus_lo = np.zeros((2, 64, 2), np.float32)
    minus_lo[:, D1:2 * D1, 0] = minus_lo[:, 2 * D1:3 * D1, 1] = -1.0
    minus_lo = minus_lo.reshape(P, 2)
    w_qkv2 = np.concatenate([l0["w_q"], l0["w_kv"]], axis=1)
    b_qkv2 = np.concatenate([l0["b_q"], l0["b_kv"]])
    return {
        "x": a["x"], "context": a["ctx_2048"], "mask1": a["mask_1x1xSxS2_fc1"][0],
        "mask2": a["mask_Bx1xSxS2_ff1"][:, 0], "keep": a["mask_Bx1x2048_bf1"],
        "ln1_s": col(l0["ln1_s"]), "ln1_b": col(l0["ln1_b"]), "w_qkv1": l0["w_qkv"],
        "b_qk1": col(l0["b_qkv"][:2 * H]), "b_v1": row(l0["b_qkv"][2 * H:]),
        "w_o1": l0["w_ao"], "b_o1": row(l0["b_ao"]),
        "ln2_s": col(l0["ln2_s"]), "ln2_b": col(l0["ln2_b"]), "w_qkv2": w_qkv2,
        "b_qk2": col(b_qkv2[:2 * H]), "b_v2": row(b_qkv2[2 * H:]),
        "w_o2": l0["w_co"], "b_o2": row(l0["b_co"]),
        "ln3_s": col(l0["ln3_s"]), "ln3_b": col(l0["ln3_b"]), "w1": l0["w1"], "b1": col(l0["b1"]),
        "w2": l0["w2"], "b2": row(l0["b2"]),
        "wq": l1["Wq"].T, "wk": l1["Wk"].T, "wv": l1["Wv"].T,
        "b_stack": b_stack, "minus_lo": minus_lo, "bv": row(l1["bv"]),
    }


def kernel(**inputs):
    import numpy as np
    import concourse.bacc as bacc
    from concourse.bass_utils import run_bass_kernel_spmd

    nc = bacc.Bacc("TRN2", target_bir_lowering=False, num_devices=1)
    arrays, args = {}, []
    for name, a in laid_out(inputs).items():
        a = np.ascontiguousarray(a)
        arrays[f"in_{name}"] = a
        args.append(nc.dram_tensor(f"in_{name}", a.shape, mybir.dt.from_np(a.dtype),
                                   kind="ExternalInput").ap())
    args.append(nc.dram_tensor("out_0", (B, S, H), F32, kind="ExternalOutput").ap())
    program(nc, *args)
    r = run_bass_kernel_spmd(nc, [arrays], core_ids=[0])
    return r.results[0]["out_0"]
```
